# Optimizing a Trainium2 kernel written in Bass

```python
import numpy as np
import jax
import jax.numpy as jnp

def _softmax(x, axis=-1):
    return jax.nn.softmax(x, axis=axis)

def _gelu(x):
    return jax.nn.gelu(x, approximate=True)

def _silu(x):
    return jax.nn.silu(x)

def _sigmoid(x):
    return jax.nn.sigmoid(x)

def _layernorm(x, axis=-1, eps=1e-05):
    m = jnp.mean(x, axis=axis, keepdims=True)
    v = jnp.var(x, axis=axis, keepdims=True)
    return (x - m) / jnp.sqrt(v + eps)

def _scatter_add(tgt, idx, src, axis=0):
    return tgt.at[idx].add(src)

def _segment_sum(src, seg, n):
    return jax.ops.segment_sum(src, seg, n)
kernel_name = 'mk_seq_postln_d1_jaxref_r8_254fb9'

def setup_inputs(seed: int=0):
    np.random.seed(seed)
    _w = jnp.asarray

    def _L0_attn_setup():
        import jax, jax.numpy as jnp
        import numpy as np
        NUM_HEADS = 16
        HIDDEN = 128
        HEAD = HIDDEN // NUM_HEADS
        key = jax.random.key(seed)
        k1, k2 = jax.random.split(key)
        embeddings = jax.random.normal(k1, (4, 256, HIDDEN), dtype=jnp.float32)
        w_qkv = jax.random.normal(k2, (HIDDEN, 3 * HIDDEN), dtype=jnp.float32) * (1.0 / np.sqrt(HIDDEN))
        return {'embeddings': embeddings, 'w_qkv': w_qkv}
    _L0_attn_in = _L0_attn_setup()

    def _L0_ffn_setup():
        import jax, jax.numpy as jnp
        import numpy as np
        B, S, D = (2, 64, 128)
        E, K, I = (16, 8, 128)
        I_SH = 128
        ROUTE_SCALE = 2.826
        key = jax.random.key(seed)
        ks = jax.random.split(key, 8)
        s = 0.02
        return {'x': jax.random.normal(ks[0], (B, S, D), dtype=jnp.float32), 'gate_w': jax.random.normal(ks[1], (E, D), dtype=jnp.float32) * s, 'expert_bias': jnp.zeros((E,), dtype=jnp.float32), 'w_gate': jax.random.normal(ks[2], (E, I, D), dtype=jnp.float32) * s, 'w_up': jax.random.normal(ks[3], (E, I, D), dtype=jnp.float32) * s, 'w_down': jax.random.normal(ks[4], (E, D, I), dtype=jnp.float32) * s, 'shared_gate_w': jax.random.normal(ks[5], (I_SH, D), dtype=jnp.float32) * s, 'shared_up_w': jax.random.normal(ks[6], (I_SH, D), dtype=jnp.float32) * s, 'shared_down_w': jax.random.normal(ks[7], (D, I_SH), dtype=jnp.float32) * s}
    _L0_ffn_in = _L0_ffn_setup()
    _d = {'L0_attn_embeddings': _L0_attn_in['embeddings'], 'L0_attn_w_qkv': _L0_attn_in['w_qkv'], 'L0_ffn_gate_w': _L0_ffn_in['gate_w'], 'L0_ffn_expert_bias': _L0_ffn_in['expert_bias'], 'L0_ffn_w_gate': _L0_ffn_in['w_gate'], 'L0_ffn_w_up': _L0_ffn_in['w_up'], 'L0_ffn_w_down': _L0_ffn_in['w_down'], 'L0_ffn_shared_gate_w': _L0_ffn_in['shared_gate_w'], 'L0_ffn_shared_up_w': _L0_ffn_in['shared_up_w'], 'L0_ffn_shared_down_w': _L0_ffn_in['shared_down_w']}
    _x0 = _d['L0_attn_embeddings']
    _d['L0_attn_embeddings'] = jax.random.normal(jax.random.fold_in(jax.random.key(seed), 1), (8, 512, 128), dtype=_x0.dtype)
    del _x0
    return _d

def reference(L0_attn_embeddings, L0_attn_w_qkv, L0_ffn_gate_w, L0_ffn_expert_bias, L0_ffn_w_gate, L0_ffn_w_up, L0_ffn_w_down, L0_ffn_shared_gate_w, L0_ffn_shared_up_w, L0_ffn_shared_down_w):

    def _L0_attn_ref(embeddings, w_qkv):
        import jax, jax.numpy as jnp
        import numpy as np
        NUM_HEADS = 16
        HIDDEN = 128
        HEAD = HIDDEN // NUM_HEADS
        b, s, h = embeddings.shape
        result = embeddings @ w_qkv
        result = result.reshape(b, s, 3, NUM_HEADS, HEAD)
        q = jnp.transpose(result[:, :, 0], (0, 2, 1, 3))
        k = jnp.transpose(result[:, :, 1], (0, 2, 1, 3))
        v = jnp.transpose(result[:, :, 2], (0, 2, 1, 3))
        scores = jnp.einsum('bnqd,bnkd->bnqk', q, k) / jnp.sqrt(jnp.float32(h))
        probs = jax.nn.softmax(scores, axis=-1)
        ctx = jnp.einsum('bnqk,bnkd->bnqd', probs, v)
        out = jnp.transpose(ctx, (0, 2, 1, 3)).reshape(b, s, h)
        return out

    def _L0_ffn_ref(x, gate_w, expert_bias, w_gate, w_up, w_down, shared_gate_w, shared_up_w, shared_down_w):
        import jax, jax.numpy as jnp
        import numpy as np
        B, S, D = (2, 64, 128)
        E, K, I = (16, 8, 128)
        I_SH = 128
        ROUTE_SCALE = 2.826
        gates = jnp.einsum('bsd,ed->bse', x, gate_w)
        scores = jax.nn.sigmoid(gates.astype(jnp.float32))
        sel_scores = scores + expert_bias
        _, inds = jax.lax.top_k(sel_scores, K)
        selected = jnp.take_along_axis(scores, inds, axis=-1)
        selected = selected / selected.sum(axis=-1, keepdims=True)
        selected = selected * ROUTE_SCALE
        onehot = jax.nn.one_hot(inds, E, dtype=selected.dtype)
        combine = jnp.einsum('bske,bsk->bse', onehot, selected)
        hg = jnp.einsum('bsd,eid->bsei', x, w_gate)
        hu = jnp.einsum('bsd,eid->bsei', x, w_up)
        h = jax.nn.silu(hg) * hu
        ye = jnp.einsum('bsei,edi->bsed', h, w_down)
        y = jnp.einsum('bsed,bse->bsd', ye, combine).astype(x.dtype)
        g = jnp.einsum('bsd,id->bsi', x, shared_gate_w)
        u = jnp.einsum('bsd,id->bsi', x, shared_up_w)
        y = y + jnp.einsum('bsi,di->bsd', jax.nn.silu(g) * u, shared_down_w)
        return y
    x = L0_attn_embeddings
    x = _layernorm(x + _L0_attn_ref(x, L0_attn_w_qkv), axis=-1)
    x = _layernorm(x + _L0_ffn_ref(x, L0_ffn_gate_w, L0_ffn_expert_bias, L0_ffn_w_gate, L0_ffn_w_up, L0_ffn_w_down, L0_ffn_shared_gate_w, L0_ffn_shared_up_w, L0_ffn_shared_down_w), axis=-1)
    return x

_drawn_inputs = setup_inputs


def setup_inputs(seed=0):
    import zlib

    import numpy as np

    out = dict(_drawn_inputs(seed))
    spreads = {'L0_ffn_expert_bias': (0.0, 0.8)}
    factors = {'L0_ffn_gate_w': 8.0,
     'L0_ffn_w_gate': 8.0,
     'L0_ffn_w_up': 8.0,
     'L0_ffn_w_down': 8.0,
     'L0_ffn_shared_gate_w': 8.0,
     'L0_ffn_shared_up_w': 8.0,
     'L0_ffn_shared_down_w': 8.0}
    for name, (base, spread) in spreads.items():
        noise = np.random.default_rng([zlib.crc32(name.encode()), seed]).standard_normal(out[name].shape)
        drawn = base * np.exp(spread * noise) if base else spread * noise
        out[name] = jnp.asarray(drawn.astype(out[name].dtype))
    for name, factor in factors.items():
        out[name] = (out[name] * factor).astype(out[name].dtype)
    return out
```

```python
import math
from contextlib import ExitStack

import concourse.bass as bass
from concourse import mybir

F32 = mybir.dt.float32
F32R = mybir.dt.float32r
ALU = mybir.AluOpType
ACT = mybir.ActivationFunctionType
AX_X = mybir.AxisListType.X

P = 128
BATCHES, SEQ, HIDDEN = 8, 512, 128
HEADS, HEAD = 16, 8
TILES = SEQ // P
GROUP = 4
GROUPS = HEADS // GROUP
UNITS = BATCHES * GROUPS
ROWS = 32
SHIFT_ROW = 3 * HEAD
AHEAD = 2
EXPERTS, TOP_K = 16, 8
NETS = EXPERTS + 1
ROUTE_SCALE = 2.826
EPS = 1e-5
STRUCK = -3e38
DMA = 16
ATT_SCALE = 1.0 / math.sqrt(HIDDEN)


def build(nc, x, xT, w_qkv, w_nets, gate_wT, expert_bias, out):
    q_rows = nc.dram_tensor("q_rows", [HEADS, ROWS, SEQ], F32).ap()
    k_rows = nc.dram_tensor("k_rows", [HEADS, ROWS, SEQ], F32).ap()
    shift_rows = nc.dram_tensor("shift_rows", [2, GROUP * TILES, P], F32).ap()
    combine_rows = nc.dram_tensor("combine_rows", [EXPERTS, SEQ], F32).ap()
    x_tiles = x.rearrange("b (t p) d -> p (b t) d", p=P)
    out_tiles = out.rearrange("b (t p) d -> p (b t) d", p=P)

    with ExitStack() as whole:
        def keep(name, shape, dt=F32):
            return whole.enter_context(nc.sbuf_tensor(name, shape, dt))

        stream = keep("stream", [P, BATCHES * TILES, HIDDEN])
        nets_high = keep("nets_high", [P, NETS, 3, P], F32R)
        nets_low = keep("nets_low", [P, NETS, 3, P], F32R)
        ident = keep("ident", [P, P])
        attention(nc, stream, nets_high, nets_low, ident, x_tiles, xT, w_qkv, w_nets,
                  q_rows, k_rows, shift_rows)
        feed_forward(nc, stream, nets_high, nets_low, ident, gate_wT, expert_bias,
                     combine_rows, out_tiles)


def attention(nc, stream, nets_high, nets_low, ident, x_tiles, xT, w_qkv, w_nets,
              q_rows, k_rows, shift_rows):
    with ExitStack() as ctx:
        def sb(name, shape, dt=F32):
            return ctx.enter_context(nc.sbuf_tensor(name, shape, dt))

        def psum(name, shape):
            return ctx.enter_context(nc.psum_tensor(name, shape, F32))

        def sem(name):
            return ctx.enter_context(nc.semaphore(name))

        q_pad = sb("q_pad", [P, GROUPS, GROUP, SEQ], F32R)
        k_aug = sb("k_aug", [P, GROUPS, SEQ], F32R)
        v_ones = sb("v_ones", [P, GROUPS, TILES, GROUP, 32])
        probs = sb("probs", [P, 2, GROUP, SEQ])
        xT_sb = sb("xT_sb", [P, SEQ])
        w_sb = sb("w_sb", [P, 3 * HIDDEN])
        qk_raw = sb("qk_raw", [P, 2, SEQ])
        qk_high = sb("qk_high", [P, 2, SEQ], F32R)
        qk_low = sb("qk_low", [P, 2, SEQ], F32R)
        v_stage = sb("v_stage", [P, TILES, HIDDEN])
        maxima = sb("maxima", [P, 2, GROUP * TILES])
        shift_raw = sb("shift_raw", [GROUP * TILES, P])
        shift = sb("shift", [GROUP * TILES, 2, P], F32R)
        context_T = sb("context_T", [P, SEQ])
        inverse = sb("inverse", [P, TILES, GROUP])
        context = sb("context", [P, 2, TILES, GROUP, HEAD])
        net_raw = sb("net_raw", [P, 3 * P])
        ones = sb("ones", [P, 3 * P])

        ps_q = [psum("ps_q0", [P, 2, SEQ]), psum("ps_q1", [P, 2, SEQ])]
        ps_k = [psum("ps_k0", [P, SEQ]), psum("ps_k1", [P, SEQ])]
        ps_ctx = psum("ps_ctx", [P, SEQ])
        ps_misc = psum("ps_misc", [P, SEQ])

        xT_loaded = sem("xT_loaded")
        w_loaded = sem("w_loaded")
        stream_loaded = sem("stream_loaded")
        pads_set = sem("pads_set")
        v_pads_set = sem("v_pads_set")
        pads_written = sem("pads_written")
        ones_set = sem("ones_set")
        ident_zeroed = sem("ident_zeroed")
        ident_set = sem("ident_set")
        qk_projected = sem("qk_projected")
        qk_highs = sem("qk_highs")
        qk_split = sem("qk_split")
        v_projected = sem("v_projected")
        v_staged = sem("v_staged")
        v_placed = sem("v_placed")
        rows_written = sem("rows_written")
        slot_loaded = [sem(f"slot_loaded{g}") for g in range(GROUPS)]
        scores_q = sem("scores_q")
        scores_q_used = sem("scores_q_used")
        maxima_turned = sem("maxima_turned")
        shift_high = sem("shift_high")
        shift_split = sem("shift_split")
        shift_written = sem("shift_written")
        shift_loaded = sem("shift_loaded")
        scores_k = sem("scores_k")
        exp_done = sem("exp_done")
        context_step = sem("context_step")
        context_copied = sem("context_copied")
        context_turned = sem("context_turned")
        context_ready = sem("context_ready")
        context_added = sem("context_added")
        net_loaded = sem("net_loaded")
        net_high = sem("net_high")
        net_split = sem("net_split")

        block = ctx.enter_context(nc.Block())

        @block.sync
        def _(sp):
            def load_xT(column):
                sp.dma_start(xT_sb[:], xT[:, bass.ds(column, SEQ)]).then_inc(xT_loaded, DMA)

            def load_slot(g):
                sp.dma_start(k_aug[:, g, :].bitcast(F32),
                             k_rows[g * GROUP:(g + 1) * GROUP].rearrange("h r s -> (h r) s")
                             ).then_inc(slot_loaded[g], DMA)
                for h in range(GROUP):
                    sp.dma_start(q_pad[h * ROWS:(h + 1) * ROWS, g, h, :].bitcast(F32),
                                 q_rows[g * GROUP + h]).then_inc(slot_loaded[g], DMA)

            def write_rows(b):
                sp.wait_ge(qk_split, 2 * b + 1)
                for part, r in ((qk_high, 0), (qk_low, 1), (qk_high, 2)):
                    sp.dma_start(q_rows[:, r * HEAD:(r + 1) * HEAD, :],
                                 part[:, 0, :].bitcast(F32)).then_inc(rows_written, DMA)
                sp.wait_ge(qk_split, 2 * b + 2)
                for part, r in ((qk_high, 0), (qk_high, 1), (qk_low, 2)):
                    sp.dma_start(k_rows[:, r * HEAD:(r + 1) * HEAD, :],
                                 part[:, 1, :].bitcast(F32)).then_inc(rows_written, DMA)

            def spread_shift(u, g):
                sp.wait_ge(shift_split, u + 1)
                sp.dma_start(shift_rows.rearrange("c m q -> m c q"),
                             shift[:].bitcast(F32)).then_inc(shift_written, DMA)
                sp.wait_ge(shift_written, DMA * (u + 1))
                for h in range(GROUP):
                    r = h * ROWS + SHIFT_ROW
                    sp.dma_start(q_pad[r:r + 2, g, h, :].bitcast(F32),
                                 shift_rows[:, h * TILES:(h + 1) * TILES, :].rearrange("c t q -> c (t q)")
                                 ).then_inc(shift_loaded, DMA)

            def body(b, first=False, last=False):
                for g in range(GROUPS):
                    u = GROUPS * b + g
                    if g == 0 and not last:
                        column = (b + 1) * SEQ
                        if not first:
                            column = sp.snap(column)
                        sp.wait_ge(v_projected, b + 1)
                        load_xT(column)
                    if not last or g == 0:
                        if not (first and g == 0):
                            sp.wait_ge(scores_k, 16 * u)
                        if g > 0:
                            sp.wait_ge(rows_written, 6 * DMA * (b + 2))
                        load_slot((g + 3) % GROUPS)
                    if not last or g < GROUPS - 1:
                        spread_shift(u + 1, (g + 1) % GROUPS)
                    if g == 0 and not last:
                        sp.wait_ge(slot_loaded[3], 5 * DMA * (b + 1))
                        write_rows(b + 1)

            load_xT(0)
            sp.dma_start(w_sb[:], w_qkv).then_inc(w_loaded, DMA)
            for c in range(4):
                n = BATCHES * TILES // 4
                sp.dma_start(stream[:, c * n:(c + 1) * n, :], x_tiles[:, c * n:(c + 1) * n, :]
                             ).then_inc(stream_loaded, DMA)
            sp.wait_ge(pads_set, 2)
            sp.dma_start(q_rows[:, SHIFT_ROW:ROWS, :], q_pad[:, 0, 0, :].bitcast(F32)).then_inc(pads_written, DMA)
            sp.dma_start(k_rows[:, SHIFT_ROW:ROWS, :], k_aug[:, 0, :].bitcast(F32)).then_inc(pads_written, DMA)
            write_rows(0)
            sp.wait_ge(pads_written, 2 * DMA)
            sp.wait_ge(rows_written, 6 * DMA)
            for g in range(3):
                load_slot(g)
            spread_shift(0, 0)
            body(0, first=True)
            with sp.Fori(1, BATCHES - 1) as b:
                body(b)
            body(BATCHES - 1, last=True)

        @block.gpsimd
        def _(pool):
            def place_v(u, g):
                pool.tensor_tensor(v_ones[:, g, :, :, 0:HEAD],
                                   v_stage[:, :, g * GROUP * HEAD:(g + 1) * GROUP * HEAD]
                                   .rearrange("p t (h e) -> p t h e", h=GROUP),
                                   ones[:, 0:HIDDEN].rearrange("p (t h e) -> p t h e", t=TILES, h=GROUP),
                                   ALU.mult).then_inc(v_placed, 1)

            def add_context(u, b, g):
                pool.wait_ge(context_ready, u + 1)
                cols = stream[:, bass.ds(b * TILES, TILES), g * GROUP * HEAD:(g + 1) * GROUP * HEAD]
                pool.tensor_tensor(cols, cols, context[:, g % 2].rearrange("p t h e -> p t (h e)"),
                                   ALU.add).then_inc(context_added, 1)

            def split_net(e):
                pool.dma_start(net_raw[:], w_nets[:, bass.ds(e * 3 * P, 3 * P)]).then_inc(net_loaded, DMA)
                high = nets_high[:, bass.ds(e, 1), :, :].rearrange("p a b c -> p (a b c)")
                low = nets_low[:, bass.ds(e, 1), :, :].rearrange("p a b c -> p (a b c)")
                pool.wait_ge(net_loaded, DMA * (e + 1))
                pool.tensor_tensor(high, net_raw[:], ones[:], ALU.mult).then_inc(net_high, 1)
                pool.wait_ge(net_high, e + 1)
                pool.tensor_tensor(low, net_raw[:], high.bitcast(F32), ALU.subtract).then_inc(net_split, 1)
                pool.wait_ge(net_split, e + 1)

            def body(b, first=False, last=False):
                for g in range(GROUPS):
                    u = GROUPS * b + g
                    if not (first and g == 0):
                        if not (last and g > 0):
                            pool.wait_ge(context_step, 4 * u)
                            pool.wait_ge(v_staged, b + 1 if g == 0 else b + 2)
                            place_v(u + 3, (g + 3) % GROUPS)
                        add_context(u - 1, b - 1 if g == 0 else b, (g + 3) % GROUPS)
                    if first:
                        for e in ((0, 1), (2,), (3,), (4,))[g]:
                            split_net(e)
                    elif not last and g in (1, 3):
                        split_net(2 * b + 3 + g // 2)

            pool.memset(ident[:], 0.0).then_inc(ident_zeroed, 1)
            pool.wait_ge(ident_zeroed, 1)
            pool.affine_select(out=ident[:], in_=ident[:], compare_op=ALU.not_equal, fill=1.0,
                               base=0, pattern=[[-1, P]], channel_multiplier=1).then_inc(ident_set, 1)
            pool.memset(v_ones[:].rearrange("p a b c d -> p (a b c d)"), 0.0).then_inc(v_pads_set, 1)
            pool.wait_ge(v_pads_set, 1)
            pool.memset(v_ones[:, :, :, :, HEAD:HEAD + 1], 1.0).then_inc(v_pads_set, 1)
            pool.memset(ones[:], 1.0).then_inc(ones_set, 1)
            pool.wait_ge(v_pads_set, 2)
            pool.wait_ge(ones_set, 1)
            pool.wait_ge(v_staged, 1)
            for g in range(GROUPS):
                place_v(g, g)
            pool.wait_ge(stream_loaded, 4 * DMA)
            body(0, first=True)
            with pool.Fori(1, BATCHES - 1) as b:
                body(b)
            body(BATCHES - 1, last=True)
            add_context(UNITS - 1, BATCHES - 1, GROUPS - 1)

        @block.scalar
        def _(act):
            def copy_context(u, wait_turned):
                act.wait_ge(context_step, 4 * (u + 1))
                if wait_turned:
                    act.wait_ge(context_turned, u)
                act.copy(context_T[:], ps_ctx[:]).then_inc(context_copied, 1)

            def round_shift(u, first):
                act.wait_ge(maxima_turned, u + 1)
                if not first:
                    act.wait_ge(shift_loaded, GROUP * DMA * u)
                act.copy(shift_raw[:], ps_misc[0:GROUP * TILES, 0:P])
                act.copy(shift[:, 0, :], ps_misc[0:GROUP * TILES, 0:P]).then_inc(shift_high, 1)

            def round_qk(b, i, first):
                act.wait_ge(qk_projected, 2 * b + i + 1)
                if not first:
                    act.wait_ge(rows_written, 6 * DMA * b)
                act.copy(qk_raw[:, i, :], ps_misc[:])
                act.copy(qk_high[:, i, :], ps_misc[:]).then_inc(qk_highs, 1)

            def stage_v(b, first):
                act.wait_ge(v_projected, b + 1)
                if not first:
                    act.wait_ge(v_placed, GROUPS * b)
                act.copy(v_stage[:].rearrange("p t d -> p (t d)"), ps_misc[:]).then_inc(v_staged, 1)

            def body(b, first=False, last=False):
                for g in range(GROUPS):
                    u = GROUPS * b + g
                    for t in range(TILES):
                        for h in range(GROUP):
                            if h == 0 and not (first and g == 0 and t < 2):
                                act.wait_ge(context_step, 4 * u + t - 1)
                            act.wait_ge(scores_k, 16 * u + 4 * t + h + 1)
                            act.activation(probs[:, t % 2, h, :], ps_k[h % 2][:], ACT.Exp,
                                           scale=ATT_SCALE).then_inc(exp_done, 1)
                            if (t, h) == (1, 0) and not (first and g == 0):
                                copy_context(u - 1, not (first and g == 1))
                            if (t, h) == (1, 1) and not (last and g == GROUPS - 1):
                                round_shift(u + 1, False)
                            if (t, h) == (2, 0) and g == 0 and not last:
                                round_qk(b + 1, 0, False)
                            if (t, h) == (3, 0) and g == 0 and not last:
                                round_qk(b + 1, 1, False)
                            if (t, h) == (3, 2) and g == 0 and not last:
                                stage_v(b + 1, False)

            round_qk(0, 0, True)
            round_qk(0, 1, True)
            stage_v(0, True)
            round_shift(0, True)
            body(0, first=True)
            with act.Fori(1, BATCHES - 1) as b:
                body(b)
            body(BATCHES - 1, last=True)
            copy_context(UNITS - 1, True)

        @block.vector
        def _(dve):
            def take_maximum(u, parity, h, j, wait_turned):
                if wait_turned:
                    dve.wait_ge(maxima_turned, u - 1)
                dve.wait_ge(scores_q, 8 * u + 2 * h + j + 1)
                dve.tensor_reduce(maxima[:, parity, TILES * h + 2 * j:TILES * h + 2 * j + 2],
                                  ps_q[j][:], AX_X, ALU.max).then_inc(scores_q_used, 1)

            def split_shift(u):
                dve.wait_ge(shift_high, u + 1)
                dve.tensor_tensor(shift[:, 1, :], shift_raw[:],
                                  shift[:, 0, :].bitcast(F32), ALU.subtract).then_inc(shift_split, 1)

            def split_qk(b, i):
                dve.wait_ge(qk_highs, 2 * b + i + 1)
                dve.tensor_tensor(qk_low[:, i, :], qk_raw[:, i, :], qk_high[:, i, :].bitcast(F32),
                                  ALU.subtract).then_inc(qk_split, 1)

            def normalise_context(u, parity, wait_added):
                turned = ps_misc[:].rearrange("p (t h c) -> p t h c", t=TILES, h=GROUP)
                dve.wait_ge(context_turned, u + 1)
                dve.reciprocal(inverse[:], turned[:, :, :, HEAD])
                dve.drain()
                if wait_added:
                    dve.wait_ge(context_added, u - 1)
                dve.tensor_tensor(context[:, parity], turned[:, :, :, 0:HEAD],
                                  inverse[:].unsqueeze(3).to_broadcast([P, TILES, GROUP, HEAD]),
                                  ALU.mult).then_inc(context_ready, 1)

            def body(b, first=False, last=False):
                for g in range(GROUPS):
                    u = GROUPS * b + g
                    maxima_of_next = not last or g < AHEAD
                    for h in range(GROUP):
                        for j in range(2):
                            if maxima_of_next:
                                take_maximum(u + AHEAD, g % 2, h, j, (h, j) == (0, 0))
                            if (h, j) == (0, 0) and g == 1 and not first and not last:
                                normalise_context(u - 2, 1, True)
                            if (h, j) == (1, 1) and not (last and g == GROUPS - 1):
                                split_shift(u + 1)
                            if (h, j) == (2, 1) and (last or g > 0):
                                normalise_context(u - 1, (g + 1) % 2, not (first and g < 3))
                            if (h, j) == (2, 1) and g == 0 and not last:
                                split_qk(b + 1, 0)
                            if (h, j) == (3, 1) and g == 0 and not last:
                                split_qk(b + 1, 1)

            dve.memset(k_aug[:].rearrange("p a b -> p (a b)").bitcast(F32), -1.0).then_inc(pads_set, 1)
            dve.memset(q_pad[:].rearrange("p a b c -> p (a b c)").bitcast(F32), 0.0).then_inc(pads_set, 1)
            split_qk(0, 0)
            split_qk(0, 1)
            for u in range(AHEAD):
                for h in range(GROUP):
                    for j in range(2):
                        take_maximum(u, u, h, j, False)
                if u == 0:
                    split_shift(0)
            body(0, first=True)
            with dve.Fori(1, BATCHES - 1) as b:
                body(b)
            body(BATCHES - 1, last=True)
            normalise_context(UNITS - 1, 1, True)

        @block.tensor
        def _(pe):
            def score_q(g, h, t):
                return pe.matmul(ps_q[t // 2][:, t % 2, :], q_pad[:, g, h, t * P:(t + 1) * P],
                                 k_aug[:, g, :], start=True, stop=True)

            def score_k(g, h, t):
                return pe.matmul(ps_k[h % 2][:], k_aug[:, g, t * P:(t + 1) * P], q_pad[:, g, h, :],
                                 start=True, stop=True)

            def weigh_values(u, g, t, wait_copied):
                pe.wait_ge(exp_done, 16 * u + 4 * t + 4)
                if t == 0:
                    pe.wait_ge(v_placed, u + 1)
                    if wait_copied:
                        pe.wait_ge(context_copied, u)
                for h in range(GROUP):
                    last = pe.matmul(ps_ctx[32 * h:32 * (h + 1), :], v_ones[:, g, t, h, :],
                                     probs[:, t % 2, h, :], start=(t == 0), stop=(t == TILES - 1))
                last.then_inc(context_step, 1)

            def turn_maxima(u, parity):
                pe.wait_ge(scores_q_used, 8 * (u + 1))
                pe.transpose(ps_misc[0:GROUP * TILES, 0:P], maxima[:, parity, :], ident[:]
                             ).then_inc(maxima_turned, 1)

            def turn_context(u):
                pe.wait_ge(context_copied, u + 1)
                for t in range(TILES):
                    last = pe.transpose(ps_misc[:, t * P:(t + 1) * P], context_T[:, t * P:(t + 1) * P], ident[:])
                last.then_inc(context_turned, 1)

            def project_qk(b, i):
                pe.matmul(ps_misc[:], w_sb[:, i * HIDDEN:(i + 1) * HIDDEN], xT_sb[:],
                          start=True, stop=True).then_inc(qk_projected, 1)

            def project_v():
                for t in range(TILES):
                    last = pe.matmul(ps_misc[:, t * P:(t + 1) * P], xT_sb[:, t * P:(t + 1) * P],
                                     w_sb[:, 2 * HIDDEN:3 * HIDDEN], start=True, stop=True)
                last.then_inc(v_projected, 1)

            def body(b, first=False, last=False):
                for g in range(GROUPS):
                    u = GROUPS * b + g
                    begun = not (first and g == 0)
                    maxima_of_next = not last or g < AHEAD
                    more = not last or g < GROUPS - 1
                    project = g == 0 and not last
                    g_next = (g + AHEAD) % GROUPS
                    for t in range(TILES):
                        for h in range(GROUP):
                            if (t, h) == (0, 0):
                                pe.wait_ge(shift_loaded, GROUP * DMA * (u + 1))
                            if begun or t > 0 or h > 1:
                                pe.wait_ge(exp_done, 16 * u + 4 * t + h - 1)
                            score_k(g, h, t).then_inc(scores_k, 1)
                            if maxima_of_next:
                                if (t, h) == (0, 0):
                                    pe.wait_ge(slot_loaded[g_next], 5 * DMA * (b + 1 + (g + AHEAD) // GROUPS))
                                if h % 2 == 0:
                                    pe.wait_ge(scores_q_used, 8 * (u + AHEAD) + 2 * t + h // 2 - 1)
                                done = score_q(g_next, t, h)
                                if h % 2 == 1:
                                    done.then_inc(scores_q, 1)
                            if (t, h) == (3, 1) and project:
                                pe.wait_ge(qk_highs, 2 * b + 4)
                                project_v()
                            if (t, h) == (2, 1) and begun and not project:
                                if more:
                                    pe.wait_ge(shift_high, u + 2)
                                else:
                                    pe.wait_ge(context_ready, u - 1)
                                turn_context(u - 1)
                        if t > 0:
                            weigh_values(u, g, t - 1, begun)
                        elif begun:
                            weigh_values(u - 1, (g + 3) % GROUPS, TILES - 1, True)
                        if t == 0 and more:
                            if not begun:
                                pe.wait_ge(shift_high, 1)
                            elif first and g == 1:
                                pe.wait_ge(v_staged, 2)
                            else:
                                pe.wait_ge(context_ready, u - 1)
                            turn_maxima(u + 1, (g + 1) % 2)
                        if t == 1 and project:
                            pe.wait_ge(shift_high, u + 2)
                            pe.wait_ge(xT_loaded, DMA * (b + 2))
                            project_qk(b + 1, 0)
                        if t == 2 and project:
                            pe.wait_ge(qk_highs, 2 * b + 3)
                            project_qk(b + 1, 1)
                        if t == 3 and project and begun:
                            pe.wait_ge(v_staged, b + 2)
                            turn_context(u - 1)

            pe.wait_ge(xT_loaded, DMA)
            pe.wait_ge(w_loaded, DMA)
            project_qk(0, 0)
            pe.wait_ge(qk_highs, 1)
            project_qk(0, 1)
            pe.wait_ge(qk_highs, 2)
            project_v()
            for u in range(AHEAD):
                pe.wait_ge(slot_loaded[u], 5 * DMA)
                for h in range(GROUP):
                    for j in range(2):
                        if 8 * u + 2 * h + j >= 2:
                            pe.wait_ge(scores_q_used, 8 * u + 2 * h + j - 1)
                        score_q(u, h, 2 * j)
                        score_q(u, h, 2 * j + 1).then_inc(scores_q, 1)
                if u == 0:
                    pe.wait_ge(ident_set, 1)
                    pe.wait_ge(v_staged, 1)
                    turn_maxima(0, 0)
            body(0, first=True)
            with pe.Fori(1, BATCHES - 1) as b:
                body(b)
            body(BATCHES - 1, last=True)
            weigh_values(UNITS - 1, GROUPS - 1, TILES - 1, True)
            pe.wait_ge(context_ready, UNITS - 1)
            turn_context(UNITS - 1)


def feed_forward(nc, stream, nets_high, nets_low, ident, gate_wT, expert_bias, combine_rows, out_tiles):
    STEPS = NETS + 1
    LAG = 3
    RING = 3
    LAST = NETS - 1

    def before(s, ring):
        n = s - ring
        while n < 0 and n + STEPS > LAST:
            n -= ring
        return (0, n) if n >= 0 else (-1, n + STEPS)

    with ExitStack() as ctx:
        def sb(name, shape, dt=F32):
            return ctx.enter_context(nc.sbuf_tensor(name, shape, dt))

        def psum(name, shape):
            return ctx.enter_context(nc.psum_tensor(name, shape, F32))

        def sem(name):
            return ctx.enter_context(nc.semaphore(name))

        x1 = sb("x1", [P, TILES, HIDDEN])
        x1T = sb("x1T", [P, SEQ])
        x1T_high = sb("x1T_high", [P, SEQ], F32R)
        x1T_low = sb("x1T_low", [P, SEQ], F32R)
        stats = sb("stats", [P, 2, TILES, 6])
        moments = sb("moments", [P, 2, TILES, 2])
        shifted = sb("shifted", [P, 2, TILES])
        scale = sb("scale", [P, 2, TILES])
        minus_half = sb("minus_half", [P, TILES])
        epsilon = sb("epsilon", [P, TILES])
        ones = sb("ones_x1", [P, TILES, HIDDEN])
        gw_sb = sb("gw_sb", [P, EXPERTS])
        bias_sb = sb("bias_sb", [P, EXPERTS])
        inv_e = sb("inv_e", [P, TILES * EXPERTS])
        gates = sb("gates", [P, TILES, EXPERTS])
        decay = sb("decay", [P, TILES, EXPERTS])
        decay1 = sb("decay1", [P, TILES, EXPERTS])
        score = sb("score", [P, TILES, EXPERTS])
        select = sb("select", [P, TILES, EXPERTS])
        top = sb("top", [P, TILES, TOP_K])
        struck = sb("struck", [P, TILES, EXPERTS])
        chosen = sb("chosen", [P, TILES, EXPERTS])
        picked = sb("picked", [P, TILES, EXPERTS])
        total = sb("total", [P, TILES])
        inverse = sb("inverse_total", [P, TILES])
        combine = sb("combine", [P, TILES, EXPERTS])
        combine_T = sb("combine_T", [EXPERTS, SEQ])
        weights = sb("weights", [P, EXPERTS, SEQ])
        silu = sb("silu", [P, 2, SEQ])
        gated = sb("gated", [P, 2, SEQ])
        hidden = sb("hidden", [P, RING, SEQ])
        hidden_high = sb("hidden_high", [P, RING, SEQ], F32R)
        hidden_low = sb("hidden_low", [P, RING, SEQ], F32R)
        yT = sb("yT", [P, SEQ])
        y_sum = sb("y_sum", [P, TILES, HIDDEN])
        result = sb("result", [P, TILES, HIDDEN])

        ps_gate = [psum("ps_gate0", [P, SEQ]), psum("ps_gate1", [P, SEQ])]
        ps_up = [psum("ps_up0", [P, SEQ]), psum("ps_up1", [P, SEQ])]
        ps_y = psum("ps_y", [P, SEQ])
        ps_x1T = psum("ps_x1T", [P, SEQ])
        ps_route = psum("ps_route", [P, SEQ])
        ps_out = psum("ps_out", [P, SEQ])

        consts_loaded = sem("consts_loaded")
        consts_set = sem("consts_set")
        moments_in = sem("moments_in")
        shifted_in = sem("shifted_in")
        scale_in = sem("scale_in")
        x1_ready = sem("x1_ready")
        x1_kept = sem("x1_kept")
        x1_turned = sem("x1_turned")
        x1T_ready = sem("x1T_ready")
        x1T_highs = sem("x1T_highs")
        x1T_split = sem("x1T_split")
        gates_ready = sem("gates_ready")
        gates_copied = sem("gates_copied")
        decayed = sem("decayed")
        combine_ready = sem("combine_ready")
        combine_turned = sem("combine_turned")
        combine_copied = sem("combine_copied")
        combine_written = sem("combine_written")
        weights_loaded = [sem(f"weights_loaded{i}") for i in range(4)]
        gate_ready = sem("gate_ready")
        up_ready = sem("up_ready")
        silu_done = sem("silu_done")
        gated_done = sem("gated_done")
        hidden_done = sem("hidden_done")
        hidden_highs = sem("hidden_highs")
        hidden_split = sem("hidden_split")
        down_done = sem("down_done")
        y_copied = sem("y_copied")
        y_turned = sem("y_turned")
        y_summed = sem("y_summed")
        moments_out = sem("moments_out")
        shifted_out = sem("shifted_out")
        scale_out = sem("scale_out")
        result_ready = sem("result_ready")
        stored = sem("stored")

        block = ctx.enter_context(nc.Block())

        LN_IN, TURN_X1, COPY_X1T, GATE, ROUTE, TURN_COMBINE, COPY_COMBINE = 1, 4, 5, 7, 9, 12, 13
        COPY_Y, TURN_Y, SUM_Y, LN_OUT = 2, 4, 5, 7

        @block.sync
        def _(sp):
            def write_combine(b, first):
                sp.wait_ge(combine_copied, b + 1)
                sp.dma_start(combine_rows, combine_T[:]).then_inc(combine_written, DMA)
                sp.wait_ge(combine_written, DMA * (b + 1))

            def load_weights(b, i, first):
                if not first:
                    sp.wait_ge(hidden_done, EXPERTS * (b - 1) + 4 * (i + 1))
                sp.dma_start(weights[:, 4 * i:4 * i + 4, :],
                             combine_rows[4 * i:4 * i + 4, :].unsqueeze(0).to_broadcast([P, 4, SEQ])
                             ).then_inc(weights_loaded[i], DMA)

            def store(b):
                tile = b * TILES if isinstance(b, int) else sp.snap(b * TILES)
                sp.wait_ge(result_ready, b + 1)
                sp.dma_start(out_tiles[:, bass.ds(tile, TILES), :], result[:]).then_inc(stored, DMA)

            def body(b, first=False, last=False):
                if not first:
                    store(b - 1)
                if not last:
                    write_combine(b + 1, False)
                    for i in range(4):
                        load_weights(b + 1, i, False)

            sp.dma_start(gw_sb[:], gate_wT).then_inc(consts_loaded, DMA)
            sp.dma_start(bias_sb[:], expert_bias.unsqueeze(0).to_broadcast([P, EXPERTS])
                         ).then_inc(consts_loaded, DMA)
            write_combine(0, True)
            for i in range(4):
                load_weights(0, i, True)
            body(0, first=True)
            with sp.Fori(1, BATCHES - 1) as b:
                body(b)
            body(BATCHES - 1, last=True)
            store(BATCHES - 1)
            sp.wait_ge(stored, DMA * BATCHES)

        @block.gpsimd
        def _(pool):
            def rstd(b, i, moments_done, shifted_done, scale_done):
                pool.wait_ge(moments_done, b + 1)
                pool.tensor_tensor(shifted[:, i, :], moments[:, i, :, 1], epsilon[:], ALU.add
                                   ).then_inc(shifted_done, 1)
                pool.wait_ge(shifted_done, b + 1)
                pool.tensor_tensor(scale[:, i, :], shifted[:, i, :], minus_half[:], ALU.pow
                                   ).then_inc(scale_done, 1)

            def keep_x1(b):
                pool.wait_ge(x1_ready, b + 1)
                pool.tensor_tensor(stream[:, bass.ds(b * TILES, TILES), :], x1[:], ones[:], ALU.mult
                                   ).then_inc(x1_kept, 1)

            def decay_gates(b):
                pool.wait_ge(gates_copied, b + 1)
                pool.tensor_tensor(decay[:].rearrange("p t e -> p (t e)"), inv_e[:],
                                   gates[:].rearrange("p t e -> p (t e)"), ALU.pow).then_inc(decayed, 1)

            def body(b, first=False, last=False):
                for s in range(STEPS):
                    if 1 <= s <= LAST:
                        e = s - 1
                        if e % 4 == 0:
                            pool.wait_ge(weights_loaded[e // 4], DMA * (b + 1))
                        pool.wait_ge(gated_done, NETS * b + s + 1)
                        db, n = before(s, RING)
                        if not (first and db < 0):
                            pool.wait_ge(hidden_split, NETS * (b + db) + n + 1)
                        pool.tensor_tensor(hidden[:, s % RING, :], gated[:, s % 2, :], weights[:, e, :],
                                           ALU.mult).then_inc(hidden_done, 1)
                    if s == LN_IN and not last:
                        rstd(b + 1, 0, moments_in, shifted_in, scale_in)
                    if s == LN_IN + 2 and not last:
                        keep_x1(b + 1)
                    if s == SUM_Y + 1 and not first:
                        rstd(b - 1, 1, moments_out, shifted_out, scale_out)
                    if s == GATE + 1 and not last:
                        decay_gates(b + 1)

            pool.memset(minus_half[:], -0.5).then_inc(consts_set, 1)
            pool.memset(inv_e[:], math.exp(-1.0)).then_inc(consts_set, 1)
            pool.memset(epsilon[:], EPS).then_inc(consts_set, 1)
            pool.memset(ones[:], 1.0).then_inc(consts_set, 1)
            pool.wait_ge(consts_set, 4)
            rstd(0, 0, moments_in, shifted_in, scale_in)
            keep_x1(0)
            decay_gates(0)
            body(0, first=True)
            with pool.Fori(1, BATCHES - 1) as b:
                body(b)
            body(BATCHES - 1, last=True)
            rstd(BATCHES - 1, 1, moments_out, shifted_out, scale_out)

        @block.scalar
        def _(act):
            def copy_x1T(b, first):
                act.wait_ge(x1_turned, b + 1)
                if not first:
                    act.wait_ge(x1T_split, b)
                    act.wait_ge(gates_ready, b)
                act.copy(x1T[:], ps_x1T[:]).then_inc(x1T_ready, 1)

            def round_x1T(b, first):
                if first:
                    act.wait_ge(x1T_ready, b + 1)
                else:
                    act.wait_ge(up_ready, NETS * b)
                act.copy(x1T_high[:], x1T[:]).then_inc(x1T_highs, 1)

            def copy_combine(b, first):
                act.wait_ge(combine_turned, b + 1)
                if not first:
                    for loaded in weights_loaded:
                        act.wait_ge(loaded, DMA * b)
                act.copy(combine_T[:], ps_route[0:EXPERTS, :]).then_inc(combine_copied, 1)

            def copy_y(b, first):
                act.wait_ge(down_done, NETS * (b + 1))
                if not first:
                    act.wait_ge(y_turned, b)
                act.copy(yT[:], ps_y[:]).then_inc(y_copied, 1)

            def round_hidden(b, n, first):
                if n == 0:
                    act.wait_ge(gated_done, NETS * b + 1)
                else:
                    act.wait_ge(hidden_done, EXPERTS * b + n)
                db, m = before(n, RING)
                if not (first and db < 0):
                    act.wait_ge(down_done, NETS * (b + db) + m + 1)
                act.copy(hidden_high[:, n % RING, :], hidden[:, n % RING, :]).then_inc(hidden_highs, 1)

            def body(b, first=False, last=False):
                for s in range(STEPS):
                    if s <= LAST:
                        act.wait_ge(gate_ready, NETS * b + s + 1)
                        db, n = before(s, 2)
                        if not (first and db < 0):
                            act.wait_ge(gated_done, NETS * (b + db) + n + 1)
                        act.activation(silu[:, s % 2, :], ps_gate[s % 2][:], ACT.Silu).then_inc(silu_done, 1)
                    if s == STEPS - 1 and not last:
                        round_x1T(b + 1, False)
                    if s >= 2:
                        round_hidden(b, s - 2, first)
                    elif s == 0 and not first:
                        round_hidden(b - 1, LAST, False)
                    if s == COPY_Y and not first:
                        copy_y(b - 1, False)
                    if s == COPY_X1T and not last:
                        copy_x1T(b + 1, False)
                    if s == COPY_COMBINE and not last:
                        copy_combine(b + 1, False)

            copy_x1T(0, True)
            round_x1T(0, True)
            copy_combine(0, True)
            body(0, first=True)
            with act.Fori(1, BATCHES - 1) as b:
                body(b)
            body(BATCHES - 1, last=True)
            round_hidden(BATCHES - 1, LAST, False)
            copy_y(BATCHES - 1, False)

        @block.vector
        def _(dve):
            def moments_of(src, i, b, moments_done):
                for t in range(TILES):
                    dve.bn_stats(stats[:, i, t, :], src(t))
                dve.drain()
                for t in range(TILES):
                    last = dve.bn_aggr(moments[:, i, t, :], stats[:, i, t, :])
                last.then_inc(moments_done, 1)

            def normalise(dst, src, i, b, scale_done, done):
                dve.wait_ge(scale_done, b + 1)
                for t in range(TILES):
                    last = dve.tensor_scalar(dst[:, t, :], src(t), moments[:, i, t, 0:1], scale[:, i, t:t + 1],
                                             ALU.subtract, ALU.mult)
                last.then_inc(done, 1)

            def stream_tile(b):
                return lambda t: stream[:, bass.ds(b * TILES + t, 1), :].rearrange("p o d -> p (o d)")

            def moments_of_stream(b):
                moments_of(stream_tile(b), 0, b, moments_in)

            def normalise_stream(b, first):
                if not first:
                    dve.wait_ge(x1_turned, b)
                    dve.wait_ge(x1_kept, b)
                normalise(x1, stream_tile(b), 0, b, scale_in, x1_ready)

            def split_x1T(b):
                dve.wait_ge(x1T_highs, b + 1)
                dve.tensor_tensor(x1T_low[:], x1T[:], x1T_high[:].bitcast(F32), ALU.subtract
                                  ).then_inc(x1T_split, 1)

            def copy_gates(b):
                dve.wait_ge(gates_ready, b + 1)
                dve.tensor_copy(gates[:].rearrange("p t e -> p (t e)"), ps_route[:, 0:TILES * EXPERTS]
                                ).then_inc(gates_copied, 1)

            def select_experts(b):
                dve.wait_ge(decayed, b + 1)
                dve.tensor_scalar(decay1[:], decay[:], 1.0, None, ALU.add)
                dve.drain()
                dve.reciprocal(score[:], decay1[:])
                dve.drain()
                dve.tensor_tensor(select[:], score[:],
                                  bias_sb[:].unsqueeze(1).to_broadcast([P, TILES, EXPERTS]), ALU.add)
                dve.drain()
                for t in range(TILES):
                    dve.max(top[:, t, :], select[:, t, :])
                dve.drain()
                for t in range(TILES):
                    dve.match_replace(struck[:, t, :], top[:, t, :], select[:, t, :], STRUCK)
                dve.drain()
                dve.tensor_tensor(chosen[:], struck[:], select[:], ALU.not_equal)
                dve.drain()
                dve.tensor_tensor(picked[:], chosen[:], score[:], ALU.mult)
                dve.drain()
                dve.tensor_reduce(total[:], picked[:], AX_X, ALU.add)
                dve.drain()
                dve.reciprocal(inverse[:], total[:])
                dve.drain()
                dve.scalar_tensor_tensor(out=combine[:], in0=picked[:], scalar=ROUTE_SCALE,
                                         in1=inverse[:].unsqueeze(2).to_broadcast([P, TILES, EXPERTS]),
                                         op0=ALU.mult, op1=ALU.mult).then_inc(combine_ready, 1)

            def sum_y(b, first):
                dve.wait_ge(y_turned, b + 1)
                dve.wait_ge(x1_kept, b + 1)
                dve.tensor_tensor(y_sum[:], ps_out[:].rearrange("p (t d) -> p t d", t=TILES),
                                  stream[:, bass.ds(b * TILES, TILES), :], ALU.add).then_inc(y_summed, 1)
                dve.drain()
                moments_of(lambda t: y_sum[:, t, :], 1, b, moments_out)

            def finish(b, first):
                if not first:
                    dve.wait_ge(stored, DMA * b)
                normalise(result, lambda t: y_sum[:, t, :], 1, b, scale_out, result_ready)

            def gate_up(b, s, first):
                dve.wait_ge(silu_done, NETS * b + s + 1)
                dve.wait_ge(up_ready, NETS * b + s + 1)
                if s == 0:
                    db, n = before(0, RING)
                    if not first:
                        dve.wait_ge(hidden_split, NETS * (b + db) + n + 1)
                    dst = hidden[:, 0, :]
                else:
                    db, n = before(s, 2)
                    if n > 0 and not (first and db < 0):
                        dve.wait_ge(hidden_done, EXPERTS * (b + db) + n)
                    dst = gated[:, s % 2, :]
                dve.tensor_tensor(dst, silu[:, s % 2, :], ps_up[s % 2][:], ALU.mult).then_inc(gated_done, 1)

            def split_hidden(b, n, first):
                dve.wait_ge(hidden_highs, NETS * b + n + 1)
                dve.tensor_tensor(hidden_low[:, n % RING, :], hidden[:, n % RING, :],
                                  hidden_high[:, n % RING, :].bitcast(F32), ALU.subtract
                                  ).then_inc(hidden_split, 1)

            def body(b, first=False, last=False):
                for s in range(STEPS):
                    if s <= LAST:
                        gate_up(b, s, first)
                    if s == STEPS - 1 and not last:
                        split_x1T(b + 1)
                    if s >= 2:
                        split_hidden(b, s - 2, first)
                    elif s == 0 and not first:
                        split_hidden(b - 1, LAST, False)
                    if s == LN_IN - 1 and not last:
                        moments_of_stream(b + 1)
                    if s == LN_IN + 1 and not last:
                        normalise_stream(b + 1, False)
                    if s == GATE and not last:
                        copy_gates(b + 1)
                    if s == ROUTE and not last:
                        select_experts(b + 1)
                    if s == SUM_Y and not first:
                        sum_y(b - 1, False)
                    if s == LN_OUT and not first:
                        finish(b - 1, False)

            dve.wait_ge(consts_loaded, 2 * DMA)
            moments_of_stream(0)
            normalise_stream(0, True)
            split_x1T(0)
            copy_gates(0)
            select_experts(0)
            body(0, first=True)
            with dve.Fori(1, BATCHES - 1) as b:
                body(b)
            body(BATCHES - 1, last=True)
            split_hidden(BATCHES - 1, LAST, False)
            sum_y(BATCHES - 1, False)
            finish(BATCHES - 1, False)

        @block.tensor
        def _(pe):
            def three_passes(dst, n, j, high, low, start, stop):
                pe.matmul(dst, nets_low[:, n, j, :], high, start=start, stop=False)
                pe.matmul(dst, nets_high[:, n, j, :], high, start=False, stop=False)
                return pe.matmul(dst, nets_high[:, n, j, :], low, start=False, stop=stop)

            def gate_up(b, s, first):
                if s == 0:
                    pe.wait_ge(x1T_highs, b + 1)
                db, n = before(s, 2)
                if not (first and db < 0):
                    pe.wait_ge(silu_done, NETS * (b + db) + n + 1)
                for j, dst, done in ((0, ps_gate[s % 2], gate_ready), (1, ps_up[s % 2], up_ready)):
                    if j == 1 and not (first and db < 0):
                        pe.wait_ge(gated_done, NETS * (b + db) + n + 1)
                    pe.matmul(dst[:], nets_low[:, s, j, :], x1T_high[:], start=True, stop=False)
                    pe.matmul(dst[:], nets_high[:, s, j, :], x1T_high[:], start=False, stop=False)
                    if s == 0 and j == 0:
                        pe.wait_ge(x1T_split, b + 1)
                    pe.matmul(dst[:], nets_high[:, s, j, :], x1T_low[:], start=False, stop=True).then_inc(done, 1)

            def down(b, n, first):
                pe.wait_ge(hidden_split, NETS * b + n + 1)
                if n == 0 and not first:
                    pe.wait_ge(y_copied, b)
                three_passes(ps_y[:], n, 2, hidden_high[:, n % RING, :], hidden_low[:, n % RING, :],
                             n == 0, n == LAST).then_inc(down_done, 1)

            def turn(dst, src, ready, ready_at, free, free_at, done):
                pe.wait_ge(ready, ready_at)
                if free is not None:
                    pe.wait_ge(free, free_at)
                for t in range(TILES):
                    last = pe.transpose(dst[:, t * P:(t + 1) * P], src[:, t * P:(t + 1) * P], ident[:])
                last.then_inc(done, 1)

            def turn_x1(b, first):
                turn(ps_x1T, x1[:].rearrange("p t d -> p (t d)"), x1_ready, b + 1,
                     None if first else x1T_ready, b, x1_turned)

            def gate(b):
                pe.wait_ge(x1T_ready, b + 1)
                for t in range(TILES):
                    last = pe.matmul(ps_route[:, t * EXPERTS:(t + 1) * EXPERTS], x1T[:, t * P:(t + 1) * P],
                                     gw_sb[:], start=True, stop=True)
                last.then_inc(gates_ready, 1)

            def turn_combine(b):
                pe.wait_ge(combine_ready, b + 1)
                for t in range(TILES):
                    last = pe.transpose(ps_route[0:EXPERTS, t * P:(t + 1) * P], combine[:, t, :], ident[:])
                last.then_inc(combine_turned, 1)

            def turn_y(b, first):
                turn(ps_out, yT[:], y_copied, b + 1, None if first else y_summed, b, y_turned)

            def body(b, first=False, last=False):
                for s in range(STEPS):
                    if s <= LAST:
                        gate_up(b, s, first)
                    if s >= LAG:
                        down(b, s - LAG, first)
                    elif s < LAG - 1 and not first:
                        down(b - 1, s + STEPS - LAG, False)
                    if s == TURN_X1 and not last:
                        turn_x1(b + 1, False)
                    if s == TURN_Y and not first:
                        turn_y(b - 1, False)
                    if s == GATE and not last:
                        pe.wait_ge(combine_copied, b + 1)
                        gate(b + 1)
                    if s == TURN_COMBINE and not last:
                        turn_combine(b + 1)

            turn_x1(0, True)
            pe.wait_ge(consts_loaded, 2 * DMA)
            gate(0)
            turn_combine(0)
            body(0, first=True)
            with pe.Fori(1, BATCHES - 1) as b:
                body(b)
            body(BATCHES - 1, last=True)
            for n in range(STEPS - LAG, NETS):
                down(BATCHES - 1, n, False)
            turn_y(BATCHES - 1, False)


def kernel(**inputs):
    import numpy as np
    import concourse.bacc as bacc
    from concourse.bass_utils import run_bass_kernel_spmd

    def array(name):
        return np.asarray(inputs[name])

    x = array("L0_attn_embeddings")
    gates = np.concatenate([array("L0_ffn_shared_gate_w")[None], array("L0_ffn_w_gate")]).transpose(2, 0, 1)
    ups = np.concatenate([array("L0_ffn_shared_up_w")[None], array("L0_ffn_w_up")]).transpose(2, 0, 1)
    downs = np.concatenate([array("L0_ffn_shared_down_w")[None], array("L0_ffn_w_down")]).transpose(2, 0, 1)
    arrays = {
        "x": x,
        "xT": x.reshape(-1, HIDDEN).T,
        "w_qkv": array("L0_attn_w_qkv"),
        "w_nets": np.stack([gates, ups, downs], axis=2).reshape(P, -1),
        "gate_wT": array("L0_ffn_gate_w").T,
        "expert_bias": array("L0_ffn_expert_bias"),
    }
    arrays = {name: np.ascontiguousarray(a) for name, a in arrays.items()}
    nc = bacc.Bacc("TRN2", target_bir_lowering=False, num_devices=1)
    args = [nc.dram_tensor(name, a.shape, mybir.dt.from_np(a.dtype), kind="ExternalInput").ap()
            for name, a in arrays.items()]
    out = nc.dram_tensor("out", x.shape, F32, kind="ExternalOutput").ap()
    build(nc, *args, out)
    r = run_bass_kernel_spmd(nc, [arrays], core_ids=[0])
    return r.results[0]["out"]
```

```python
import math
from contextlib import ExitStack

import concourse.bass as bass
from concourse import mybir

F32 = mybir.dt.float32
F32R = mybir.dt.float32r
ALU = mybir.AluOpType
ACT = mybir.ActivationFunctionType
AX_X = mybir.AxisListType.X

P = 128
BATCHES, SEQ, HIDDEN = 8, 512, 128
HEADS, HEAD = 16, 8
TILES = SEQ // P
GROUP = 4
GROUPS = HEADS // GROUP
UNITS = BATCHES * GROUPS
ROWS = 32
SHIFT_ROW = 3 * HEAD
AHEAD = 2
SCORES = GROUPS * TILES * GROUP
TURN = 56
SCORE_SLOT = [i % 3 if i < TURN else (TURN - i) % 3 for i in range(SCORES)]
EXPERTS, TOP_K = 16, 8
NETS = EXPERTS + 1
ROUTE_SCALE = 2.826
EPS = 1e-5
STRUCK = -3e38
DMA = 16
ATT_SCALE = 1.0 / math.sqrt(HIDDEN)


def slot_user_before(i):
    j = i - 1
    while SCORE_SLOT[j % SCORES] != SCORE_SLOT[i]:
        j -= 1
    return j


def build(nc, x, xT, w_qkv, w_nets, gate_wT, expert_bias, out):
    q_rows = nc.dram_tensor("q_rows", [HEADS, ROWS, SEQ], F32).ap()
    k_rows = nc.dram_tensor("k_rows", [HEADS, ROWS, SEQ], F32).ap()
    shift_rows = nc.dram_tensor("shift_rows", [2, GROUP * TILES, P], F32).ap()
    combine_rows = nc.dram_tensor("combine_rows", [EXPERTS, SEQ], F32).ap()
    x_tiles = x.rearrange("b (t p) d -> p (b t) d", p=P)
    out_tiles = out.rearrange("b (t p) d -> p (b t) d", p=P)

    with ExitStack() as whole:
        def keep(name, shape, dt=F32):
            return whole.enter_context(nc.sbuf_tensor(name, shape, dt))

        stream = keep("stream", [P, BATCHES * TILES, HIDDEN])
        nets_high = keep("nets_high", [P, NETS, 3, P], F32R)
        nets_low = keep("nets_low", [P, NETS, 3, P], F32R)
        ident = keep("ident", [P, P])
        r = RouteState(nc, whole, combine_rows)
        attention(nc, r, stream, nets_high, nets_low, ident, x_tiles, xT, w_qkv, w_nets,
                  gate_wT, expert_bias, q_rows, k_rows, shift_rows)
        feed_forward(nc, r, stream, nets_high, nets_low, ident, out_tiles)


class RouteState:

    def __init__(self, nc, ctx, combine_rows):
        def sb(name, shape, dt=F32):
            return ctx.enter_context(nc.sbuf_tensor(name, shape, dt))

        def sem(name):
            return ctx.enter_context(nc.semaphore(name))

        self.combine_rows = combine_rows
        self.x1 = sb("x1", [P, TILES, HIDDEN])
        self.x1T = sb("x1T", [P, SEQ])
        self.x1T_high = sb("x1T_high", [P, SEQ], F32R)
        self.x1T_low = sb("x1T_low", [P, SEQ], F32R)
        self.stats = sb("stats", [P, 2, TILES, 6])
        self.moments = sb("moments", [P, 2, TILES, 2])
        self.shifted = sb("shifted", [P, 2, TILES])
        self.scale = sb("scale", [P, 2, TILES])
        self.minus_half = sb("minus_half", [P, TILES])
        self.epsilon = sb("epsilon", [P, TILES])
        self.ones = sb("ones", [P, SEQ])
        self.gate_w = sb("gate_w", [P, EXPERTS])
        self.bias = sb("bias", [P, EXPERTS])
        self.decay = sb("decay", [P, TILES, EXPERTS])
        self.decay1 = sb("decay1", [P, TILES, EXPERTS])
        self.score = sb("score", [P, TILES, EXPERTS])
        self.select = sb("select", [P, TILES, EXPERTS])
        self.top = sb("top", [P, TILES, TOP_K])
        self.struck = sb("struck", [P, TILES, EXPERTS])
        self.chosen = sb("chosen", [P, TILES, EXPERTS])
        self.picked = sb("picked", [P, TILES, EXPERTS])
        self.total = sb("total", [P, TILES])
        self.inverse = sb("inverse_total", [P, TILES])
        self.combine = sb("combine", [P, TILES, EXPERTS])
        self.combine_T = sb("combine_T", [EXPERTS, SEQ])
        self.weights = sb("weights", [P, EXPERTS, SEQ])
        self.consts_set = sem("consts_set")
        self.consts_loaded = sem("consts_loaded")
        self.moments_ready = [sem("moments_in"), sem("moments_out")]
        self.shifted_ready = [sem("shifted_in"), sem("shifted_out")]
        self.scale_ready = [sem("scale_in"), sem("scale_out")]
        self.x1_ready = sem("x1_ready")
        self.x1_kept = sem("x1_kept")
        self.x1_turned = sem("x1_turned")
        self.x1T_ready = sem("x1T_ready")
        self.x1T_highs = sem("x1T_highs")
        self.x1T_split = sem("x1T_split")
        self.gates_ready = sem("gates_ready")
        self.decayed = sem("decayed")
        self.combine_ready = sem("combine_ready")
        self.combine_turned = sem("combine_turned")
        self.combine_copied = sem("combine_copied")
        self.combine_written = sem("combine_written")
        self.weights_loaded = [sem(f"weights_loaded{i}") for i in range(4)]


def take_moments(dve, r, tile, i):
    for t in range(TILES):
        dve.bn_stats(r.stats[:, i, t, :], tile(t))
    dve.drain()
    for t in range(TILES):
        last = dve.bn_aggr(r.moments[:, i, t, :], r.stats[:, i, t, :])
    last.then_inc(r.moments_ready[i], 1)


def take_scale(pool, r, b, i):
    pool.wait_ge(r.moments_ready[i], b + 1)
    pool.tensor_tensor(r.shifted[:, i, :], r.moments[:, i, :, 1], r.epsilon[:], ALU.add
                       ).then_inc(r.shifted_ready[i], 1)
    pool.wait_ge(r.shifted_ready[i], b + 1)
    pool.tensor_tensor(r.scale[:, i, :], r.shifted[:, i, :], r.minus_half[:], ALU.pow
                       ).then_inc(r.scale_ready[i], 1)


def normalise(dve, r, dst, tile, b, i, done):
    dve.wait_ge(r.scale_ready[i], b + 1)
    for t in range(TILES):
        last = dve.tensor_scalar(dst[:, t, :], tile(t), r.moments[:, i, t, 0:1], r.scale[:, i, t:t + 1],
                                 ALU.subtract, ALU.mult)
    last.then_inc(done, 1)


def stream_tile(stream, b):
    return lambda t: stream[:, bass.ds(b * TILES + t, 1), :].rearrange("p o d -> p (o d)")


def normalise_stream(dve, r, stream, b, first):
    if not first:
        dve.wait_ge(r.x1_turned, b)
        dve.wait_ge(r.x1_kept, b)
    normalise(dve, r, r.x1, stream_tile(stream, b), b, 0, r.x1_ready)


def keep_x1(pool, r, stream, b):
    pool.wait_ge(r.x1_ready, b + 1)
    pool.tensor_tensor(stream[:, bass.ds(b * TILES, TILES), :], r.x1[:],
                       r.ones[:].rearrange("p (t d) -> p t d", t=TILES), ALU.mult).then_inc(r.x1_kept, 1)


def turn_x1(pe, r, ident, dst, b):
    pe.wait_ge(r.x1_ready, b + 1)
    for t in range(TILES):
        last = pe.transpose(dst[:, t * P:(t + 1) * P], r.x1[:, t, :], ident[:])
    last.then_inc(r.x1_turned, 1)


def copy_x1T(act, r, src, b, first):
    act.wait_ge(r.x1_turned, b + 1)
    if not first:
        act.wait_ge(r.x1T_split, b)
        act.wait_ge(r.gates_ready, b)
    act.copy(r.x1T[:], src[:]).then_inc(r.x1T_ready, 1)


def round_x1T(act, r):
    act.copy(r.x1T_high[:], r.x1T[:]).then_inc(r.x1T_highs, 1)


def split_x1T(dve, r, b):
    dve.wait_ge(r.x1T_highs, b + 1)
    dve.tensor_tensor(r.x1T_low[:], r.x1T[:], r.x1T_high[:].bitcast(F32), ALU.subtract
                      ).then_inc(r.x1T_split, 1)


def gate(pe, r, dst, b):
    pe.wait_ge(r.x1T_ready, b + 1)
    for t in range(TILES):
        last = pe.matmul(dst[:, t * EXPERTS:(t + 1) * EXPERTS], r.x1T[:, t * P:(t + 1) * P],
                         r.gate_w[:], start=True, stop=True)
    last.then_inc(r.gates_ready, 1)


def decay_gates(act, r, src, b):
    act.wait_ge(r.gates_ready, b + 1)
    act.activation(r.decay[:].rearrange("p t e -> p (t e)"), src[:, 0:TILES * EXPERTS], ACT.Exp,
                   scale=-1.0).then_inc(r.decayed, 1)


def select_experts(dve, r, b, part):
    if part == 0:
        dve.wait_ge(r.decayed, b + 1)
        dve.tensor_scalar(r.decay1[:], r.decay[:], 1.0, None, ALU.add)
        dve.drain()
        dve.reciprocal(r.score[:], r.decay1[:])
        dve.drain()
        dve.tensor_tensor(r.select[:], r.score[:],
                          r.bias[:].unsqueeze(1).to_broadcast([P, TILES, EXPERTS]), ALU.add)
        dve.drain()
    if part == 1:
        for t in range(TILES):
            dve.max(r.top[:, t, :], r.select[:, t, :])
        dve.drain()
        for t in range(TILES):
            dve.match_replace(r.struck[:, t, :], r.top[:, t, :], r.select[:, t, :], STRUCK)
        dve.drain()
    if part == 2:
        dve.tensor_tensor(r.chosen[:], r.struck[:], r.select[:], ALU.not_equal)
        dve.drain()
        dve.tensor_tensor(r.picked[:], r.chosen[:], r.score[:], ALU.mult)
        dve.drain()
        dve.tensor_reduce(r.total[:], r.picked[:], AX_X, ALU.add)
        dve.drain()
        dve.reciprocal(r.inverse[:], r.total[:])
        dve.drain()
        dve.scalar_tensor_tensor(out=r.combine[:], in0=r.picked[:], scalar=ROUTE_SCALE,
                                 in1=r.inverse[:].unsqueeze(2).to_broadcast([P, TILES, EXPERTS]),
                                 op0=ALU.mult, op1=ALU.mult).then_inc(r.combine_ready, 1)


def turn_combine(pe, r, ident, dst, b):
    pe.wait_ge(r.combine_ready, b + 1)
    for t in range(TILES):
        last = pe.transpose(dst[0:EXPERTS, t * P:(t + 1) * P], r.combine[:, t, :], ident[:])
    last.then_inc(r.combine_turned, 1)


def copy_combine(act, r, src, b, first):
    act.wait_ge(r.combine_turned, b + 1)
    if not first:
        for loaded in r.weights_loaded:
            act.wait_ge(loaded, DMA * b)
    act.copy(r.combine_T[:], src[0:EXPERTS, :]).then_inc(r.combine_copied, 1)


def write_combine(sp, r, b):
    sp.wait_ge(r.combine_copied, b + 1)
    sp.dma_start(r.combine_rows, r.combine_T[:]).then_inc(r.combine_written, DMA)
    sp.wait_ge(r.combine_written, DMA * (b + 1))


def load_weights(sp, r, i):
    sp.dma_start(r.weights[:, 4 * i:4 * i + 4, :],
                 r.combine_rows[4 * i:4 * i + 4, :].unsqueeze(0).to_broadcast([P, 4, SEQ])
                 ).then_inc(r.weights_loaded[i], DMA)


def attention(nc, r, stream, nets_high, nets_low, ident, x_tiles, xT, w_qkv, w_nets,
              gate_wT, expert_bias, q_rows, k_rows, shift_rows):
    with ExitStack() as ctx:
        def sb(name, shape, dt=F32):
            return ctx.enter_context(nc.sbuf_tensor(name, shape, dt))

        def psum(name, shape):
            return ctx.enter_context(nc.psum_tensor(name, shape, F32))

        def sem(name):
            return ctx.enter_context(nc.semaphore(name))

        q_pad = sb("q_pad", [P, GROUPS, GROUP, SEQ], F32R)
        k_aug = sb("k_aug", [P, GROUPS, SEQ], F32R)
        v_ones = sb("v_ones", [P, GROUPS, TILES, GROUP, 32])
        probs = sb("probs", [P, 2, GROUP, SEQ])
        xT_sb = sb("xT_sb", [P, SEQ])
        w_sb = sb("w_sb", [P, 3 * HIDDEN])
        qk_raw = sb("qk_raw", [P, 2, SEQ])
        qk_high = sb("qk_high", [P, 2, SEQ], F32R)
        qk_low = sb("qk_low", [P, 2, SEQ], F32R)
        v_stage = sb("v_stage", [P, TILES, HIDDEN])
        maxima = sb("maxima", [P, 2, GROUP * TILES])
        shift_raw = sb("shift_raw", [GROUP * TILES, P])
        shift = sb("shift", [GROUP * TILES, 2, P], F32R)
        context_T = sb("context_T", [P, SEQ])
        inverse = sb("inverse", [P, TILES, GROUP])
        context = sb("context", [P, 2, TILES, GROUP, HEAD])
        net_raw = sb("net_raw", [P, 3 * P])


        ps_q = [psum(f"ps_q{i}", [P, SEQ]) for i in range(3)]
        ps_k = [psum(f"ps_k{i}", [P, SEQ]) for i in range(3)]
        ps_ctx = psum("ps_ctx", [P, SEQ])
        ps_misc = psum("ps_misc", [P, SEQ])

        xT_loaded = sem("xT_loaded")
        w_loaded = sem("w_loaded")
        stream_loaded = sem("stream_loaded")
        pads_set = sem("pads_set")
        q_pads_set = sem("q_pads_set")
        v_pads_set = sem("v_pads_set")
        pads_written = sem("pads_written")
        ident_zeroed = sem("ident_zeroed")
        ident_set = sem("ident_set")
        qk_projected = sem("qk_projected")
        qk_highs = sem("qk_highs")
        qk_split = sem("qk_split")
        v_projected = sem("v_projected")
        v_staged = sem("v_staged")
        v_placed = sem("v_placed")
        rows_written = sem("rows_written")
        slot_loaded = [sem(f"slot_loaded{g}") for g in range(GROUPS)]
        scores_q = sem("scores_q")
        scores_q_used = sem("scores_q_used")
        maxima_turned = sem("maxima_turned")
        shift_high = sem("shift_high")
        shift_split = sem("shift_split")
        shift_written = sem("shift_written")
        shift_loaded = sem("shift_loaded")
        scores_k = sem("scores_k")
        exp_done = sem("exp_done")
        context_step = sem("context_step")
        context_copied = sem("context_copied")
        context_turned = sem("context_turned")
        context_ready = sem("context_ready")
        context_added = sem("context_added")
        net_loaded = sem("net_loaded")
        net_high = sem("net_high")
        net_split = sem("net_split")

        block = ctx.enter_context(nc.Block())

        @block.sync
        def _(sp):
            def load_xT(column):
                sp.dma_start(xT_sb[:], xT[:, bass.ds(column, SEQ)]).then_inc(xT_loaded, DMA)

            def load_slot(g):
                sp.dma_start(k_aug[:, g, :].bitcast(F32),
                             k_rows[g * GROUP:(g + 1) * GROUP].rearrange("h r s -> (h r) s")
                             ).then_inc(slot_loaded[g], DMA)
                for h in range(GROUP):
                    sp.dma_start(q_pad[h * ROWS:(h + 1) * ROWS, g, h, :].bitcast(F32),
                                 q_rows[g * GROUP + h]).then_inc(slot_loaded[g], DMA)

            def write_rows(b):
                def write(rows, part, i, r):
                    sp.dma_start(rows[:, r * HEAD:(r + 1) * HEAD, :], part[:, i, :].bitcast(F32)
                                 ).then_inc(rows_written, DMA)

                sp.wait_ge(qk_highs, 2 * b + 1)
                write(q_rows, qk_high, 0, 0)
                write(q_rows, qk_high, 0, 2)
                sp.wait_ge(qk_split, 2 * b + 1)
                write(q_rows, qk_low, 0, 1)
                sp.wait_ge(qk_highs, 2 * b + 2)
                write(k_rows, qk_high, 1, 0)
                write(k_rows, qk_high, 1, 1)
                sp.wait_ge(qk_split, 2 * b + 2)
                write(k_rows, qk_low, 1, 2)

            def spread_shift(u, g):
                sp.wait_ge(shift_split, u + 1)
                sp.dma_start(shift_rows.rearrange("c m q -> m c q"),
                             shift[:].bitcast(F32)).then_inc(shift_written, DMA)
                sp.wait_ge(shift_written, DMA * (u + 1))
                for h in range(GROUP):
                    r = h * ROWS + SHIFT_ROW
                    sp.dma_start(q_pad[r:r + 2, g, h, :].bitcast(F32),
                                 shift_rows[:, h * TILES:(h + 1) * TILES, :].rearrange("c t q -> c (t q)")
                                 ).then_inc(shift_loaded, DMA)

            def body(b, first=False, last=False):
                for g in range(GROUPS):
                    u = GROUPS * b + g
                    if g == 0 and not last:
                        column = (b + 1) * SEQ
                        if not first:
                            column = sp.snap(column)
                        sp.wait_ge(v_projected, b + 1)
                        load_xT(column)
                    if not last or g == 0:
                        if not (first and g == 0):
                            sp.wait_ge(scores_k, 16 * u)
                        if g > 0:
                            sp.wait_ge(rows_written, 6 * DMA * (b + 2))
                        load_slot((g + 3) % GROUPS)
                    if not last or g < GROUPS - 1:
                        spread_shift(u + 1, (g + 1) % GROUPS)
                    if g == 0 and not last:
                        sp.wait_ge(slot_loaded[3], 5 * DMA * (b + 1))
                        write_rows(b + 1)

            load_xT(0)
            sp.dma_start(w_sb[:], w_qkv).then_inc(w_loaded, DMA)
            sp.wait_ge(pads_set, 2)
            sp.dma_start(q_rows[:, SHIFT_ROW:ROWS, :], q_pad[:, 0, 0, :].bitcast(F32)).then_inc(pads_written, DMA)
            sp.dma_start(k_rows[:, SHIFT_ROW:ROWS, :], k_aug[:, 0, :].bitcast(F32)).then_inc(pads_written, DMA)
            write_rows(0)
            sp.wait_ge(pads_written, 2 * DMA)
            sp.wait_ge(rows_written, 6 * DMA)
            load_slot(0)
            sp.wait_ge(q_pads_set, 1)
            load_slot(1)
            load_slot(2)
            for c in range(4):
                n = BATCHES * TILES // 4
                sp.dma_start(stream[:, c * n:(c + 1) * n, :], x_tiles[:, c * n:(c + 1) * n, :]
                             ).then_inc(stream_loaded, DMA)
            sp.dma_start(r.gate_w[:], gate_wT).then_inc(r.consts_loaded, DMA)
            sp.dma_start(r.bias[:], expert_bias.unsqueeze(0).to_broadcast([P, EXPERTS])
                         ).then_inc(r.consts_loaded, DMA)
            spread_shift(0, 0)
            body(0, first=True)
            with sp.Fori(1, BATCHES - 1) as b:
                body(b)
            body(BATCHES - 1, last=True)
            write_combine(sp, r, 0)
            for i in range(4):
                load_weights(sp, r, i)

        @block.gpsimd
        def _(pool):
            def place_v(u, g):
                pool.tensor_tensor(v_ones[:, g, :, :, 0:HEAD],
                                   v_stage[:, :, g * GROUP * HEAD:(g + 1) * GROUP * HEAD]
                                   .rearrange("p t (h e) -> p t h e", h=GROUP),
                                   r.ones[:, 0:HIDDEN].rearrange("p (t h e) -> p t h e", t=TILES, h=GROUP),
                                   ALU.mult).then_inc(v_placed, 1)

            def add_context(u, b, g):
                pool.wait_ge(context_ready, u + 1)
                cols = stream[:, bass.ds(b * TILES, TILES), g * GROUP * HEAD:(g + 1) * GROUP * HEAD]
                pool.tensor_tensor(cols, cols, context[:, g % 2].rearrange("p t h e -> p t (h e)"),
                                   ALU.add).then_inc(context_added, 1)

            def split_net(e):
                pool.dma_start(net_raw[:], w_nets[:, bass.ds(e * 3 * P, 3 * P)]).then_inc(net_loaded, DMA)
                high = nets_high[:, bass.ds(e, 1), :, :].rearrange("p a b c -> p (a b c)")
                low = nets_low[:, bass.ds(e, 1), :, :].rearrange("p a b c -> p (a b c)")
                pool.wait_ge(net_loaded, DMA * (e + 1))
                pool.tensor_tensor(high, net_raw[:], r.ones[:, 0:3 * P], ALU.mult).then_inc(net_high, 1)
                pool.wait_ge(net_high, e + 1)
                pool.tensor_tensor(low, net_raw[:], high.bitcast(F32), ALU.subtract).then_inc(net_split, 1)
                pool.wait_ge(net_split, e + 1)

            def body(b, first=False, last=False):
                for g in range(GROUPS):
                    u = GROUPS * b + g
                    if not (first and g == 0):
                        if not (last and g > 0):
                            pool.wait_ge(context_step, 4 * u)
                            pool.wait_ge(v_staged, b + 1 if g == 0 else b + 2)
                            place_v(u + 3, (g + 3) % GROUPS)
                        add_context(u - 1, b - 1 if g == 0 else b, (g + 3) % GROUPS)
                    if first:
                        for e in ((0, 1), (2,), (3,), (4,))[g]:
                            split_net(e)
                    elif not last and g in (1, 3):
                        split_net(2 * b + 3 + g // 2)
                    elif last and g == 1:
                        take_scale(pool, r, 0, 0)
                        keep_x1(pool, r, stream, 0)

            pool.memset(q_pad[:, 1:, :, :].rearrange("p a b c -> p (a b c)").bitcast(F32), 0.0
                        ).then_inc(q_pads_set, 1)
            pool.memset(ident[:], 0.0).then_inc(ident_zeroed, 1)
            pool.wait_ge(ident_zeroed, 1)
            pool.affine_select(out=ident[:], in_=ident[:], compare_op=ALU.not_equal, fill=1.0,
                               base=0, pattern=[[-1, P]], channel_multiplier=1).then_inc(ident_set, 1)
            pool.memset(v_ones[:].rearrange("p a b c d -> p (a b c d)"), 0.0).then_inc(v_pads_set, 1)
            pool.wait_ge(v_pads_set, 1)
            pool.memset(v_ones[:, :, :, :, HEAD:HEAD + 1], 1.0).then_inc(v_pads_set, 1)
            pool.memset(r.ones[:], 1.0).then_inc(r.consts_set, 1)
            pool.memset(r.minus_half[:], -0.5).then_inc(r.consts_set, 1)
            pool.memset(r.epsilon[:], EPS).then_inc(r.consts_set, 1)
            pool.wait_ge(v_pads_set, 2)
            pool.wait_ge(r.consts_set, 3)
            pool.wait_ge(v_staged, 1)
            for g in range(GROUPS):
                place_v(g, g)
            pool.wait_ge(stream_loaded, 4 * DMA)
            body(0, first=True)
            with pool.Fori(1, BATCHES - 1) as b:
                body(b)
            body(BATCHES - 1, last=True)
            add_context(UNITS - 1, BATCHES - 1, GROUPS - 1)

        @block.scalar
        def _(act):
            def copy_context(u, wait_turned):
                act.wait_ge(context_step, 4 * (u + 1))
                if wait_turned:
                    act.wait_ge(context_turned, u)
                act.copy(context_T[:], ps_ctx[:]).then_inc(context_copied, 1)

            def round_shift(u, first):
                act.wait_ge(maxima_turned, u + 1)
                if not first:
                    act.wait_ge(shift_loaded, GROUP * DMA * u)
                act.copy(shift_raw[:], ps_misc[0:GROUP * TILES, 0:P])
                act.copy(shift[:, 0, :], ps_misc[0:GROUP * TILES, 0:P]).then_inc(shift_high, 1)

            def round_qk(b, i, src, first):
                act.wait_ge(qk_projected, 2 * b + i + 1)
                if not first:
                    act.wait_ge(rows_written, 6 * DMA * b)
                act.copy(qk_raw[:, i, :], src[:])
                act.copy(qk_high[:, i, :], src[:]).then_inc(qk_highs, 1)

            def stage_v(b, src, first):
                act.wait_ge(v_projected, b + 1)
                if not first:
                    act.wait_ge(v_placed, GROUPS * b)
                act.copy(v_stage[:].rearrange("p t d -> p (t d)"), src[:]).then_inc(v_staged, 1)

            def body(b, first=False, last=False):
                for g in range(GROUPS):
                    u = GROUPS * b + g
                    for t in range(TILES):
                        for h in range(GROUP):
                            i = 16 * g + 4 * t + h
                            if h == 0 and not (first and g == 0 and t < 2):
                                act.wait_ge(context_step, 4 * u + t - 1)
                            act.wait_ge(scores_k, SCORES * b + i + 1)
                            act.activation(probs[:, t % 2, h, :], ps_k[SCORE_SLOT[i]][:], ACT.Exp,
                                           scale=ATT_SCALE).then_inc(exp_done, 1)
                            if (t, h) == (0, 3) and not (last and g == GROUPS - 1):
                                round_shift(u + 1, False)
                            if (t, h) == (1, 0) and not (first and g == 0):
                                copy_context(u - 1, not (first and g == 1))
                            if (t, h) == (1, 3) and g == 0 and not last:
                                round_qk(b + 1, 0, ps_misc, False)
                            if (t, h) == (2, 3) and g == 0 and not last:
                                round_qk(b + 1, 1, ps_misc, False)
                            if (g, t, h) == (2, 1, 3) and last:
                                copy_x1T(act, r, ps_misc, 0, True)
                            if (g, t, h) == (2, 2, 1) and last:
                                act.wait_ge(r.x1T_ready, 1)
                                round_x1T(act, r)
                            if (g, t, h) == (2, 3, 3) and last:
                                decay_gates(act, r, ps_misc, 0)
                            if (g, t, h) == (3, 1, 3) and last:
                                copy_combine(act, r, ps_misc, 0, True)
                            if (t, h) == (3, 2) and g == 0 and not last:
                                stage_v(b + 1, ps_misc, False)

            round_qk(0, 0, ps_misc, True)
            round_qk(0, 1, ps_ctx, True)
            stage_v(0, ps_k[0], True)
            round_shift(0, True)
            body(0, first=True)
            with act.Fori(1, BATCHES - 1) as b:
                body(b)
            body(BATCHES - 1, last=True)
            copy_context(UNITS - 1, True)

        @block.vector
        def _(dve):
            def take_maximum(u, b, i, parity, wait_turned):
                if wait_turned:
                    dve.wait_ge(maxima_turned, u - 1)
                dve.wait_ge(scores_q, SCORES * b + i + 1)
                dve.tensor_reduce(maxima[:, parity, i % 16:i % 16 + 1], ps_q[SCORE_SLOT[i % SCORES]][:],
                                  AX_X, ALU.max).then_inc(scores_q_used, 1)

            def split_shift(u):
                dve.wait_ge(shift_high, u + 1)
                dve.tensor_tensor(shift[:, 1, :], shift_raw[:],
                                  shift[:, 0, :].bitcast(F32), ALU.subtract).then_inc(shift_split, 1)

            def split_qk(b, i):
                dve.wait_ge(qk_highs, 2 * b + i + 1)
                dve.tensor_tensor(qk_low[:, i, :], qk_raw[:, i, :], qk_high[:, i, :].bitcast(F32),
                                  ALU.subtract).then_inc(qk_split, 1)

            def normalise_context(u, parity, wait_added):
                turned = ps_misc[:].rearrange("p (t h c) -> p t h c", t=TILES, h=GROUP)
                dve.wait_ge(context_turned, u + 1)
                dve.reciprocal(inverse[:], turned[:, :, :, HEAD])
                dve.drain()
                if wait_added:
                    dve.wait_ge(context_added, u - 1)
                dve.tensor_tensor(context[:, parity], turned[:, :, :, 0:HEAD],
                                  inverse[:].unsqueeze(3).to_broadcast([P, TILES, GROUP, HEAD]),
                                  ALU.mult).then_inc(context_ready, 1)

            def body(b, first=False, last=False):
                for g in range(GROUPS):
                    u = GROUPS * b + g
                    maxima_of_next = not last or g < AHEAD
                    for i in range(16):
                        if maxima_of_next:
                            take_maximum(u + AHEAD, b, 16 * (g + AHEAD) + i, g % 2, i == 0)
                        if i == 0 and g == 1 and not first and not last:
                            normalise_context(u - 2, 1, True)
                        if i == 3 and not (last and g == GROUPS - 1):
                            split_shift(u + 1)
                        if i == 11 and (last or g > 0):
                            normalise_context(u - 1, (g + 1) % 2, not (first and g < 3))
                        if i == 9 and g == 0 and not last:
                            split_qk(b + 1, 0)
                        if i == 13 and g == 0 and not last:
                            split_qk(b + 1, 1)
                        if i == 3 and g == 1 and last:
                            take_moments(dve, r, stream_tile(stream, 0), 0)
                        if i == 15 and g == 1 and last:
                            normalise_stream(dve, r, stream, 0, True)
                        if i == 11 and g == 2 and last:
                            split_x1T(dve, r, 0)
                            for part in range(3):
                                select_experts(dve, r, 0, part)

            dve.memset(k_aug[:, 0, :].bitcast(F32), -1.0).then_inc(pads_set, 1)
            dve.memset(q_pad[:, 0, :, :].rearrange("p b c -> p (b c)").bitcast(F32), 0.0).then_inc(pads_set, 1)
            split_qk(0, 0)
            split_qk(0, 1)
            for u in range(AHEAD):
                for i in range(16):
                    take_maximum(u, 0, 16 * u + i, u, False)
                if u == 0:
                    split_shift(0)
            body(0, first=True)
            with dve.Fori(1, BATCHES - 1) as b:
                body(b)
            body(BATCHES - 1, last=True)
            normalise_context(UNITS - 1, 1, True)

        @block.tensor
        def _(pe):
            def score_q(i):
                g, h, t = i // 16, i // 4 % 4, i % 4
                return pe.matmul(ps_q[SCORE_SLOT[i]][:], q_pad[:, g, h, t * P:(t + 1) * P],
                                 k_aug[:, g, :], start=True, stop=True).then_inc(scores_q, 1)

            def score_k(i):
                g, t, h = i // 16, i // 4 % 4, i % 4
                return pe.matmul(ps_k[SCORE_SLOT[i]][:], k_aug[:, g, t * P:(t + 1) * P], q_pad[:, g, h, :],
                                 start=True, stop=True).then_inc(scores_k, 1)

            def weigh_values(u, g, t, wait_copied):
                pe.wait_ge(exp_done, 16 * u + 4 * (t + 1))
                if t == 0:
                    pe.wait_ge(v_placed, u + 1)
                    if wait_copied:
                        pe.wait_ge(context_copied, u)
                for h in range(GROUP):
                    last = pe.matmul(ps_ctx[32 * h:32 * (h + 1), :], v_ones[:, g, t, h, :],
                                     probs[:, t % 2, h, :], start=(t == 0), stop=(t == TILES - 1))
                last.then_inc(context_step, 1)

            def turn_maxima(u, parity):
                pe.wait_ge(scores_q_used, 16 * (u + 1))
                pe.transpose(ps_misc[0:GROUP * TILES, 0:P], maxima[:, parity, :], ident[:]
                             ).then_inc(maxima_turned, 1)

            def turn_context(u):
                pe.wait_ge(context_copied, u + 1)
                for t in range(TILES):
                    last = pe.transpose(ps_misc[:, t * P:(t + 1) * P], context_T[:, t * P:(t + 1) * P], ident[:])
                last.then_inc(context_turned, 1)

            def project_qk(i, dst):
                pe.matmul(dst[:], w_sb[:, i * HIDDEN:(i + 1) * HIDDEN], xT_sb[:],
                          start=True, stop=True).then_inc(qk_projected, 1)

            def project_v(dst):
                for t in range(TILES):
                    last = pe.matmul(dst[:, t * P:(t + 1) * P], xT_sb[:, t * P:(t + 1) * P],
                                     w_sb[:, 2 * HIDDEN:3 * HIDDEN], start=True, stop=True)
                last.then_inc(v_projected, 1)

            def body(b, first=False, last=False):
                for g in range(GROUPS):
                    u = GROUPS * b + g
                    begun = not (first and g == 0)
                    maxima_of_next = not last or g < AHEAD
                    more = not last or g < GROUPS - 1
                    project = g == 0 and not last
                    g_next = (g + AHEAD) % GROUPS
                    for t in range(TILES):
                        for h in range(GROUP):
                            if (t, h) == (0, 0):
                                pe.wait_ge(shift_loaded, GROUP * DMA * (u + 1))
                            i = 16 * g + 4 * t + h
                            before = slot_user_before(i)
                            if not first or before >= 0:
                                pe.wait_ge(exp_done, SCORES * b + before + 1)
                            score_k(i)
                            if maxima_of_next:
                                if (t, h) == (0, 0):
                                    pe.wait_ge(slot_loaded[g_next], 5 * DMA * (b + 1 + (g + AHEAD) // GROUPS))
                                over, i = divmod(i + 16 * AHEAD, SCORES)
                                before = slot_user_before(i)
                                pe.wait_ge(scores_q_used, SCORES * (b + over) + before + 1)
                                score_q(i)
                            if (t, h) == (1, 2) and project:
                                pe.wait_ge(shift_high, u + 2)
                                pe.wait_ge(xT_loaded, DMA * (b + 2))
                                project_qk(0, ps_misc)
                            if (g, t, h) == (2, 1, 2) and last:
                                pe.wait_ge(shift_high, u + 2)
                                turn_x1(pe, r, ident, ps_misc, 0)
                            if (g, t, h) == (2, 3, 2) and last:
                                pe.wait_ge(context_ready, u)
                                pe.wait_ge(r.consts_loaded, 2 * DMA)
                                gate(pe, r, ps_misc, 0)
                            if (g, t, h) == (3, 1, 2) and last:
                                turn_combine(pe, r, ident, ps_misc, 0)
                            if (t, h) == (2, 2) and project:
                                pe.wait_ge(qk_highs, 2 * b + 3)
                                project_qk(1, ps_misc)
                            if (t, h) == (0, 2 if g != 1 else 3) and more:
                                if not begun:
                                    pe.wait_ge(shift_high, 1)
                                elif first and g == 1:
                                    pe.wait_ge(v_staged, 2)
                                else:
                                    pe.wait_ge(context_ready, u - 1)
                                turn_maxima(u + 1, (g + 1) % 2)
                            if (t, h) == (3, 1) and project:
                                pe.wait_ge(qk_highs, 2 * b + 4)
                                project_v(ps_misc)
                            if (t, h) == (2, 1) and begun and not project:
                                if last and g == 2:
                                    pe.wait_ge(r.x1T_ready, 1)
                                elif last and g == 3:
                                    pe.wait_ge(r.combine_copied, 1)
                                elif more:
                                    pe.wait_ge(shift_high, u + 2)
                                else:
                                    pe.wait_ge(context_ready, u - 1)
                                turn_context(u - 1)
                        if t > 0:
                            weigh_values(u, g, t - 1, begun)
                        elif begun:
                            weigh_values(u - 1, (g + 3) % GROUPS, TILES - 1, True)
                        if t == 3 and project and begun:
                            pe.wait_ge(v_staged, b + 2)
                            turn_context(u - 1)

            pe.wait_ge(xT_loaded, DMA)
            pe.wait_ge(w_loaded, DMA)
            project_qk(0, ps_misc)
            project_qk(1, ps_ctx)
            project_v(ps_k[0])
            for u in range(AHEAD):
                pe.wait_ge(slot_loaded[u], 5 * DMA)
                for i in range(16 * u, 16 * (u + 1)):
                    if i >= 3:
                        pe.wait_ge(scores_q_used, slot_user_before(i) + 1)
                    score_q(i)
                if u == 0:
                    pe.wait_ge(ident_set, 1)
                    pe.wait_ge(v_staged, 1)
                    turn_maxima(0, 0)
            body(0, first=True)
            with pe.Fori(1, BATCHES - 1) as b:
                body(b)
            body(BATCHES - 1, last=True)
            weigh_values(UNITS - 1, GROUPS - 1, TILES - 1, True)
            pe.wait_ge(context_ready, UNITS - 1)
            turn_context(UNITS - 1)


def feed_forward(nc, r, stream, nets_high, nets_low, ident, out_tiles):
    STEPS = NETS + 1
    LAG = 4
    UP_RING = 3
    RING = 6
    LAST = NETS - 1

    def before(s, ring):
        n = s - ring
        while n < 0 and n + STEPS > LAST:
            n -= ring
        return (0, n) if n >= 0 else (-1, n + STEPS)

    with ExitStack() as ctx:
        def sb(name, shape, dt=F32):
            return ctx.enter_context(nc.sbuf_tensor(name, shape, dt))

        def psum(name, shape):
            return ctx.enter_context(nc.psum_tensor(name, shape, F32))

        def sem(name):
            return ctx.enter_context(nc.semaphore(name))

        silu = sb("silu", [P, UP_RING, SEQ])
        gated = sb("gated", [P, UP_RING, SEQ])
        hidden = sb("hidden", [P, RING, SEQ])
        hidden_high = sb("hidden_high", [P, RING, SEQ], F32R)
        hidden_low = sb("hidden_low", [P, RING, SEQ], F32R)
        yT = sb("yT", [P, SEQ])
        y_sum = sb("y_sum", [P, TILES, HIDDEN])
        result = sb("result", [P, TILES, HIDDEN])

        ps_gate = [psum("ps_gate0", [P, SEQ]), psum("ps_gate1", [P, SEQ])]
        ps_up = [psum(f"ps_up{i}", [P, SEQ]) for i in range(UP_RING)]
        ps_y = psum("ps_y", [P, SEQ])
        ps_route = psum("ps_route", [P, SEQ])
        ps_out = psum("ps_out", [P, SEQ])

        gate_ready = sem("gate_ready")
        up_ready = sem("up_ready")
        silu_done = sem("silu_done")
        gated_done = sem("gated_done")
        hidden_done = sem("hidden_done")
        hidden_highs = sem("hidden_highs")
        hidden_split = sem("hidden_split")
        down_done = sem("down_done")
        y_copied = sem("y_copied")
        y_turned = sem("y_turned")
        y_summed = sem("y_summed")
        result_ready = sem("result_ready")
        stored = sem("stored")

        block = ctx.enter_context(nc.Block())

        LN_IN, TURN_X1, COPY_X1T, GATE, ROUTE, TURN_COMBINE, COPY_COMBINE = 1, 5, 5, 6, 7, 14, 14
        COPY_Y, TURN_Y, SUM_Y, LN_OUT = 3, 5, 6, 14

        @block.sync
        def _(sp):
            def store(b):
                tile = b * TILES if isinstance(b, int) else sp.snap(b * TILES)
                sp.wait_ge(result_ready, b + 1)
                sp.dma_start(out_tiles[:, bass.ds(tile, TILES), :], result[:]).then_inc(stored, DMA)

            def body(b, first=False, last=False):
                if not first:
                    store(b - 1)
                if not last:
                    write_combine(sp, r, b + 1)
                    for i in range(4):
                        sp.wait_ge(hidden_done, EXPERTS * b + 4 * (i + 1))
                        load_weights(sp, r, i)

            body(0, first=True)
            with sp.Fori(1, BATCHES - 1) as b:
                body(b)
            body(BATCHES - 1, last=True)
            store(BATCHES - 1)
            sp.wait_ge(stored, DMA * BATCHES)

        @block.gpsimd
        def _(pool):
            def body(b, first=False, last=False):
                for s in range(STEPS):
                    if 1 <= s <= LAST:
                        e = s - 1
                        if e % 4 == 0:
                            pool.wait_ge(r.weights_loaded[e // 4], DMA * (b + 1))
                        pool.wait_ge(gated_done, NETS * b + s + 1)
                        db, n = before(s, RING)
                        if not (first and db < 0):
                            pool.wait_ge(hidden_split, NETS * (b + db) + n + 1)
                        pool.tensor_tensor(hidden[:, s % RING, :], gated[:, s % UP_RING, :], r.weights[:, e, :],
                                           ALU.mult).then_inc(hidden_done, 1)
                    if s == LN_IN and not last:
                        take_scale(pool, r, b + 1, 0)
                    if s == LN_IN + 2 and not last:
                        keep_x1(pool, r, stream, b + 1)
                    if s == SUM_Y + 1 and not first:
                        take_scale(pool, r, b - 1, 1)

            body(0, first=True)
            with pool.Fori(1, BATCHES - 1) as b:
                body(b)
            body(BATCHES - 1, last=True)
            take_scale(pool, r, BATCHES - 1, 1)

        @block.scalar
        def _(act):
            def copy_y(b, first):
                act.wait_ge(down_done, NETS * (b + 1))
                if not first:
                    act.wait_ge(y_turned, b)
                act.copy(yT[:], ps_y[:]).then_inc(y_copied, 1)

            def round_hidden(b, n, first):
                if n == 0:
                    act.wait_ge(gated_done, NETS * b + 1)
                else:
                    act.wait_ge(hidden_done, EXPERTS * b + n)
                db, m = before(n, RING)
                if not (first and db < 0):
                    act.wait_ge(down_done, NETS * (b + db) + m + 1)
                act.copy(hidden_high[:, n % RING, :], hidden[:, n % RING, :]).then_inc(hidden_highs, 1)

            def body(b, first=False, last=False):
                for s in range(STEPS):
                    if s <= LAST:
                        act.wait_ge(gate_ready, NETS * b + s + 1)
                        db, n = before(s, UP_RING)
                        if not (first and db < 0):
                            act.wait_ge(gated_done, NETS * (b + db) + n + 1)
                        act.activation(silu[:, s % UP_RING, :], ps_gate[s % 2][:], ACT.Silu).then_inc(silu_done, 1)
                    if s == STEPS - 1 and not last:
                        act.wait_ge(up_ready, NETS * (b + 1))
                        round_x1T(act, r)
                    if s >= 2:
                        round_hidden(b, s - 2, first)
                    elif s == 0 and not first:
                        round_hidden(b - 1, LAST, False)
                    if s == COPY_Y and not first:
                        copy_y(b - 1, False)
                    if s == COPY_X1T and not last:
                        copy_x1T(act, r, ps_route, b + 1, False)
                    if s == COPY_COMBINE and not last:
                        copy_combine(act, r, ps_route, b + 1, False)
                    if s == GATE + 1 and not last:
                        decay_gates(act, r, ps_route, b + 1)

            body(0, first=True)
            with act.Fori(1, BATCHES - 1) as b:
                body(b)
            body(BATCHES - 1, last=True)
            round_hidden(BATCHES - 1, LAST, False)
            copy_y(BATCHES - 1, False)

        @block.vector
        def _(dve):
            def sum_y(b, first):
                dve.wait_ge(y_turned, b + 1)
                dve.wait_ge(r.x1_kept, b + 1)
                dve.tensor_tensor(y_sum[:], ps_out[:].rearrange("p (t d) -> p t d", t=TILES),
                                  stream[:, bass.ds(b * TILES, TILES), :], ALU.add).then_inc(y_summed, 1)
                dve.drain()
                take_moments(dve, r, lambda t: y_sum[:, t, :], 1)

            def finish(b, first):
                if not first:
                    dve.wait_ge(stored, DMA * b)
                normalise(dve, r, result, lambda t: y_sum[:, t, :], b, 1, result_ready)

            def gate_up(b, s, first):
                dve.wait_ge(silu_done, NETS * b + s + 1)
                dve.wait_ge(up_ready, NETS * b + s + 1)
                if s == 0:
                    db, n = before(0, RING)
                    if not first:
                        dve.wait_ge(hidden_split, NETS * (b + db) + n + 1)
                    dst = hidden[:, 0, :]
                else:
                    db, n = before(s, UP_RING)
                    if n > 0 and not (first and db < 0):
                        dve.wait_ge(hidden_done, EXPERTS * (b + db) + n)
                    dst = gated[:, s % UP_RING, :]
                dve.tensor_tensor(dst, silu[:, s % UP_RING, :], ps_up[s % UP_RING][:], ALU.mult).then_inc(gated_done, 1)

            def split_hidden(b, n, first):
                dve.wait_ge(hidden_highs, NETS * b + n + 1)
                dve.tensor_tensor(hidden_low[:, n % RING, :], hidden[:, n % RING, :],
                                  hidden_high[:, n % RING, :].bitcast(F32), ALU.subtract
                                  ).then_inc(hidden_split, 1)

            def body(b, first=False, last=False):
                for s in range(STEPS):
                    if s <= LAST:
                        gate_up(b, s, first)
                    if s == STEPS - 1 and not last:
                        split_x1T(dve, r, b + 1)
                    if s >= 2:
                        split_hidden(b, s - 2, first)
                    elif s == 0 and not first:
                        split_hidden(b - 1, LAST, False)
                    if s == LN_IN - 1 and not last:
                        take_moments(dve, r, stream_tile(stream, b + 1), 0)
                    if s == LN_IN + 1 and not last:
                        normalise_stream(dve, r, stream, b + 1, False)
                    if s in (ROUTE, ROUTE + 2, ROUTE + 4) and not last:
                        select_experts(dve, r, b + 1, (s - ROUTE) // 2)
                    if s == SUM_Y and not first:
                        sum_y(b - 1, False)
                    if s == LN_OUT and not first:
                        finish(b - 1, False)

            body(0, first=True)
            with dve.Fori(1, BATCHES - 1) as b:
                body(b)
            body(BATCHES - 1, last=True)
            split_hidden(BATCHES - 1, LAST, False)
            sum_y(BATCHES - 1, False)
            finish(BATCHES - 1, False)

        @block.tensor
        def _(pe):
            def three_passes(dst, n, j, high, low, start, stop):
                pe.matmul(dst, nets_low[:, n, j, :], high, start=start, stop=False)
                pe.matmul(dst, nets_high[:, n, j, :], high, start=False, stop=False)
                return pe.matmul(dst, nets_high[:, n, j, :], low, start=False, stop=stop)

            def gate_up(b, s, first):
                if s == 0:
                    pe.wait_ge(r.x1T_highs, b + 1)
                db, n = before(s, 2)
                if not (first and db < 0):
                    pe.wait_ge(silu_done, NETS * (b + db) + n + 1)
                def low_weights(j, dst):
                    pe.matmul(dst[:], nets_low[:, s, j, :], r.x1T_high[:], start=True, stop=False)

                def high_weights(j, dst, x, stop):
                    return pe.matmul(dst[:], nets_high[:, s, j, :], x[:], start=False, stop=stop)

                ps_g, ps_u = ps_gate[s % 2], ps_up[s % UP_RING]
                low_weights(0, ps_g)
                high_weights(0, ps_g, r.x1T_high, False)
                if s > 0:
                    high_weights(0, ps_g, r.x1T_low, True).then_inc(gate_ready, 1)
                db, n = before(s, UP_RING)
                if not (first and db < 0):
                    pe.wait_ge(gated_done, NETS * (b + db) + n + 1)
                low_weights(1, ps_u)
                high_weights(1, ps_u, r.x1T_high, False)
                if s == 0:
                    pe.wait_ge(r.x1T_split, b + 1)
                    high_weights(0, ps_g, r.x1T_low, True).then_inc(gate_ready, 1)
                high_weights(1, ps_u, r.x1T_low, True).then_inc(up_ready, 1)

            def down(b, n, first):
                pe.wait_ge(hidden_split, NETS * b + n + 1)
                if n == 0 and not first:
                    pe.wait_ge(y_copied, b)
                three_passes(ps_y[:], n, 2, hidden_high[:, n % RING, :], hidden_low[:, n % RING, :],
                             n == 0, n == LAST).then_inc(down_done, 1)

            def turn_y(b, first):
                pe.wait_ge(y_copied, b + 1)
                if not first:
                    pe.wait_ge(y_summed, b)
                for t in range(TILES):
                    last = pe.transpose(ps_out[:, t * P:(t + 1) * P], yT[:, t * P:(t + 1) * P], ident[:])
                last.then_inc(y_turned, 1)

            def body(b, first=False, last=False):
                for s in range(STEPS):
                    if s <= LAST:
                        gate_up(b, s, first)
                    if s >= LAG:
                        down(b, s - LAG, first)
                    elif s < LAG - 1 and not first:
                        down(b - 1, s + STEPS - LAG, False)
                    if s == TURN_X1 and not last:
                        pe.wait_ge(r.combine_copied, b + 1)
                        turn_x1(pe, r, ident, ps_route, b + 1)
                    if s == TURN_Y and not first:
                        turn_y(b - 1, False)
                    if s == GATE and not last:
                        gate(pe, r, ps_route, b + 1)
                    if s == TURN_COMBINE and not last:
                        turn_combine(pe, r, ident, ps_route, b + 1)

            body(0, first=True)
            with pe.Fori(1, BATCHES - 1) as b:
                body(b)
            body(BATCHES - 1, last=True)
            for n in range(STEPS - LAG, NETS):
                down(BATCHES - 1, n, False)
            turn_y(BATCHES - 1, False)


def kernel(**inputs):
    import numpy as np
    import concourse.bacc as bacc
    from concourse.bass_utils import run_bass_kernel_spmd

    def array(name):
        return np.asarray(inputs[name])

    x = array("L0_attn_embeddings")
    gates = np.concatenate([array("L0_ffn_shared_gate_w")[None], array("L0_ffn_w_gate")]).transpose(2, 0, 1)
    ups = np.concatenate([array("L0_ffn_shared_up_w")[None], array("L0_ffn_w_up")]).transpose(2, 0, 1)
    downs = np.concatenate([array("L0_ffn_shared_down_w")[None], array("L0_ffn_w_down")]).transpose(2, 0, 1)
    arrays = {
        "x": x,
        "xT": x.reshape(-1, HIDDEN).T,
        "w_qkv": array("L0_attn_w_qkv"),
        "w_nets": np.stack([gates, ups, downs], axis=2).reshape(P, -1),
        "gate_wT": array("L0_ffn_gate_w").T,
        "expert_bias": array("L0_ffn_expert_bias"),
    }
    arrays = {name: np.ascontiguousarray(a) for name, a in arrays.items()}
    nc = bacc.Bacc("TRN2", target_bir_lowering=False, num_devices=1)
    args = [nc.dram_tensor(name, a.shape, mybir.dt.from_np(a.dtype), kind="ExternalInput").ap()
            for name, a in arrays.items()]
    out = nc.dram_tensor("out", x.shape, F32, kind="ExternalOutput").ap()
    build(nc, *args, out)
    r = run_bass_kernel_spmd(nc, [arrays], core_ids=[0])
    return r.results[0]["out"]
```

```python
import math
from contextlib import ExitStack

import concourse.bass as bass
from concourse import mybir

F32 = mybir.dt.float32
F32R = mybir.dt.float32r
ALU = mybir.AluOpType
ACT = mybir.ActivationFunctionType
AX_X = mybir.AxisListType.X

P = 128
BATCHES, SEQ, HIDDEN = 8, 512, 128
HEADS, HEAD = 16, 8
TILES = SEQ // P
GROUP = 4
GROUPS = HEADS // GROUP
UNITS = BATCHES * GROUPS
PAIR = 2
ROWS = 32
SHIFT_ROW = 3 * HEAD
AHEAD = 2
UNIT = TILES * GROUP
SCORES = GROUPS * UNIT
TURN = 56
SCORE_SLOT = [i % 3 if i < TURN else (TURN - i) % 3 for i in range(SCORES)]
V_COLUMN = [j * ROWS // PAIR for j in range(PAIR)]
EXPERTS, TOP_K = 16, 8
NETS = EXPERTS + 1
ROUTE_SCALE = 2.826
EPS = 1e-5
STRUCK = -3e38
DMA = 16
ATT_SCALE = 1.0 / math.sqrt(HIDDEN)


def slot_user_before(i):
    j = i - 1
    while SCORE_SLOT[j % SCORES] != SCORE_SLOT[i]:
        j -= 1
    return j


def slot_loads(g, times):
    first_apart = GROUP - 1 if g == 0 else 0
    return DMA * ((1 + GROUP) * times - first_apart)


def build(nc, x, xT, w_qkv, w_nets, gate_wT, expert_bias, out):
    q_rows = nc.dram_tensor("q_rows", [HEADS, ROWS, SEQ], F32).ap()
    k_rows = nc.dram_tensor("k_rows", [HEADS, ROWS, SEQ], F32).ap()
    shift_rows = nc.dram_tensor("shift_rows", [2, GROUP * TILES, P], F32).ap()
    combine_rows = nc.dram_tensor("combine_rows", [EXPERTS, SEQ], F32).ap()
    x_tiles = x.rearrange("b (t p) d -> p (b t) d", p=P)
    out_tiles = out.rearrange("b (t p) d -> p (b t) d", p=P)

    with ExitStack() as whole:
        def keep(name, shape, dt=F32):
            return whole.enter_context(nc.sbuf_tensor(name, shape, dt))

        stream = keep("stream", [P, BATCHES * TILES, HIDDEN])
        nets_high = keep("nets_high", [P, NETS, 3, P], F32R)
        nets_low = keep("nets_low", [P, NETS, 3, P], F32R)
        ident = keep("ident", [P, P])
        r = RouteState(nc, whole, combine_rows)
        c = ContextState(nc, whole)
        attention(nc, r, c, stream, nets_high, nets_low, ident, x_tiles, xT, w_qkv, w_nets,
                  gate_wT, expert_bias, q_rows, k_rows, shift_rows)
        feed_forward(nc, r, c, stream, nets_high, nets_low, ident, out_tiles)


class RouteState:

    def __init__(self, nc, ctx, combine_rows):
        def sb(name, shape, dt=F32):
            return ctx.enter_context(nc.sbuf_tensor(name, shape, dt))

        def sem(name):
            return ctx.enter_context(nc.semaphore(name))

        self.combine_rows = combine_rows
        self.x1 = sb("x1", [P, TILES, HIDDEN])
        self.x1T = sb("x1T", [P, SEQ])
        self.x1T_high = sb("x1T_high", [P, SEQ], F32R)
        self.x1T_low = sb("x1T_low", [P, SEQ], F32R)
        self.stats = sb("stats", [P, 2, TILES, 6])
        self.moments = sb("moments", [P, 2, TILES, 2])
        self.shifted = sb("shifted", [P, 2, TILES])
        self.scale = sb("scale", [P, 2, TILES])
        self.minus_half = sb("minus_half", [P, TILES])
        self.epsilon = sb("epsilon", [P, TILES])
        self.ones = sb("ones", [P, SEQ])
        self.gate_w = sb("gate_w", [P, EXPERTS])
        self.bias = sb("bias", [P, EXPERTS])
        self.decay = sb("decay", [P, TILES, EXPERTS])
        self.decay1 = sb("decay1", [P, TILES, EXPERTS])
        self.score = sb("score", [P, TILES, EXPERTS])
        self.select = sb("select", [P, TILES, EXPERTS])
        self.top = sb("top", [P, TILES, TOP_K])
        self.struck = sb("struck", [P, TILES, EXPERTS])
        self.chosen = sb("chosen", [P, TILES, EXPERTS])
        self.picked = sb("picked", [P, TILES, EXPERTS])
        self.total = sb("total", [P, TILES])
        self.inverse = sb("inverse_total", [P, TILES])
        self.combine = sb("combine", [P, TILES, EXPERTS])
        self.combine_T = sb("combine_T", [EXPERTS, SEQ])
        self.weights = sb("weights", [P, EXPERTS, SEQ])
        self.consts_set = sem("consts_set")
        self.consts_loaded = sem("consts_loaded")
        self.moments_ready = [sem("moments_in"), sem("moments_out")]
        self.shifted_ready = [sem("shifted_in"), sem("shifted_out")]
        self.scale_ready = [sem("scale_in"), sem("scale_out")]
        self.x1_ready = sem("x1_ready")
        self.x1_kept = sem("x1_kept")
        self.x1_turned = sem("x1_turned")
        self.x1T_ready = sem("x1T_ready")
        self.x1T_highs = sem("x1T_highs")
        self.x1T_split = sem("x1T_split")
        self.gates_ready = sem("gates_ready")
        self.decayed = sem("decayed")
        self.combine_ready = sem("combine_ready")
        self.combine_turned = sem("combine_turned")
        self.combine_copied = sem("combine_copied")
        self.combine_written = sem("combine_written")
        self.weights_loaded = [sem(f"weights_loaded{i}") for i in range(4)]


class ContextState:

    def __init__(self, nc, ctx):
        self.context_T = ctx.enter_context(nc.sbuf_tensor("context_T", [P, SEQ], F32))
        self.inverse = ctx.enter_context(nc.sbuf_tensor("inverse", [P, PAIR, TILES, GROUP], F32))
        self.context = ctx.enter_context(nc.sbuf_tensor("context", [P, TILES, PAIR, GROUP, HEAD], F32))
        self.ps_turned = ctx.enter_context(nc.psum_tensor("ps_turned", [P, SEQ], F32))
        self.copied = ctx.enter_context(nc.semaphore("context_copied"))
        self.turned = ctx.enter_context(nc.semaphore("context_turned"))
        self.ready = ctx.enter_context(nc.semaphore("context_ready"))
        self.added = ctx.enter_context(nc.semaphore("context_added"))


def turn_context(pe, c, ident, pair):
    pe.wait_ge(c.copied, pair + 1)
    for t in range(TILES):
        last = pe.transpose(c.ps_turned[:, t * P:(t + 1) * P], c.context_T[:, t * P:(t + 1) * P], ident[:])
    last.then_inc(c.turned, 1)


def normalise_context(dve, c, pair, wait_added):
    turned = c.ps_turned[:].rearrange("p (t h c) -> p t h c", t=TILES, h=GROUP)
    dve.wait_ge(c.turned, pair + 1)
    for j, at in enumerate(V_COLUMN):
        dve.reciprocal(c.inverse[:, j], turned[:, :, :, at + HEAD])
    dve.drain()
    if wait_added:
        dve.wait_ge(c.added, pair)
    for j, at in enumerate(V_COLUMN):
        last = dve.tensor_tensor(c.context[:, :, j], turned[:, :, :, at:at + HEAD],
                                 c.inverse[:, j].unsqueeze(3).to_broadcast([P, TILES, GROUP, HEAD]),
                                 ALU.mult)
    last.then_inc(c.ready, 1)


def add_context(pool, c, stream, pair, b, second):
    pool.wait_ge(c.ready, pair + 1)
    n = PAIR * GROUP * HEAD
    cols = stream[:, bass.ds(b * TILES, TILES), second * n:(second + 1) * n]
    pool.tensor_tensor(cols, cols, c.context[:].rearrange("p t j h e -> p t (j h e)"),
                       ALU.add).then_inc(c.added, 1)


def take_moments(dve, r, tile, i):
    for t in range(TILES):
        dve.bn_stats(r.stats[:, i, t, :], tile(t))
    dve.drain()
    for t in range(TILES):
        last = dve.bn_aggr(r.moments[:, i, t, :], r.stats[:, i, t, :])
    last.then_inc(r.moments_ready[i], 1)


def take_scale(pool, r, b, i):
    pool.wait_ge(r.moments_ready[i], b + 1)
    pool.tensor_tensor(r.shifted[:, i, :], r.moments[:, i, :, 1], r.epsilon[:], ALU.add
                       ).then_inc(r.shifted_ready[i], 1)
    pool.wait_ge(r.shifted_ready[i], b + 1)
    pool.tensor_tensor(r.scale[:, i, :], r.shifted[:, i, :], r.minus_half[:], ALU.pow
                       ).then_inc(r.scale_ready[i], 1)


def normalise(dve, r, dst, tile, b, i, done):
    dve.wait_ge(r.scale_ready[i], b + 1)
    for t in range(TILES):
        last = dve.tensor_scalar(dst[:, t, :], tile(t), r.moments[:, i, t, 0:1], r.scale[:, i, t:t + 1],
                                 ALU.subtract, ALU.mult)
    last.then_inc(done, 1)


def stream_tile(stream, b):
    return lambda t: stream[:, bass.ds(b * TILES + t, 1), :].rearrange("p o d -> p (o d)")


def normalise_stream(dve, r, stream, b, first):
    if not first:
        dve.wait_ge(r.x1_turned, b)
        dve.wait_ge(r.x1_kept, b)
    normalise(dve, r, r.x1, stream_tile(stream, b), b, 0, r.x1_ready)


def keep_x1(pool, r, stream, b):
    pool.wait_ge(r.x1_ready, b + 1)
    pool.tensor_tensor(stream[:, bass.ds(b * TILES, TILES), :], r.x1[:],
                       r.ones[:].rearrange("p (t d) -> p t d", t=TILES), ALU.mult).then_inc(r.x1_kept, 1)


def turn_x1(pe, r, ident, dst, b):
    pe.wait_ge(r.x1_ready, b + 1)
    for t in range(TILES):
        last = pe.transpose(dst[:, t * P:(t + 1) * P], r.x1[:, t, :], ident[:])
    last.then_inc(r.x1_turned, 1)


def copy_x1T(act, r, src, b, first):
    act.wait_ge(r.x1_turned, b + 1)
    if not first:
        act.wait_ge(r.x1T_split, b)
        act.wait_ge(r.gates_ready, b)
    act.copy(r.x1T[:], src[:]).then_inc(r.x1T_ready, 1)


def round_x1T(act, r):
    act.copy(r.x1T_high[:], r.x1T[:]).then_inc(r.x1T_highs, 1)


def split_x1T(dve, r, b):
    dve.wait_ge(r.x1T_highs, b + 1)
    dve.tensor_tensor(r.x1T_low[:], r.x1T[:], r.x1T_high[:].bitcast(F32), ALU.subtract
                      ).then_inc(r.x1T_split, 1)


def gate(pe, r, dst, b):
    pe.wait_ge(r.x1T_ready, b + 1)
    for t in range(TILES):
        last = pe.matmul(dst[:, t * EXPERTS:(t + 1) * EXPERTS], r.x1T[:, t * P:(t + 1) * P],
                         r.gate_w[:], start=True, stop=True)
    last.then_inc(r.gates_ready, 1)


def decay_gates(act, r, src, b):
    act.wait_ge(r.gates_ready, b + 1)
    act.activation(r.decay[:].rearrange("p t e -> p (t e)"), src[:, 0:TILES * EXPERTS], ACT.Exp,
                   scale=-1.0).then_inc(r.decayed, 1)


def select_experts(dve, r, b, part):
    if part == 0:
        dve.wait_ge(r.decayed, b + 1)
        dve.tensor_scalar(r.decay1[:], r.decay[:], 1.0, None, ALU.add)
        dve.drain()
        dve.reciprocal(r.score[:], r.decay1[:])
        dve.drain()
        dve.tensor_tensor(r.select[:], r.score[:],
                          r.bias[:].unsqueeze(1).to_broadcast([P, TILES, EXPERTS]), ALU.add)
        dve.drain()
    if part == 1:
        for t in range(TILES):
            dve.max(r.top[:, t, :], r.select[:, t, :])
        dve.drain()
        for t in range(TILES):
            dve.match_replace(r.struck[:, t, :], r.top[:, t, :], r.select[:, t, :], STRUCK)
        dve.drain()
    if part == 2:
        dve.tensor_tensor(r.chosen[:], r.struck[:], r.select[:], ALU.not_equal)
        dve.drain()
        dve.tensor_tensor(r.picked[:], r.chosen[:], r.score[:], ALU.mult)
        dve.drain()
        dve.tensor_reduce(r.total[:], r.picked[:], AX_X, ALU.add)
        dve.drain()
        dve.reciprocal(r.inverse[:], r.total[:])
        dve.drain()
        dve.scalar_tensor_tensor(out=r.combine[:], in0=r.picked[:], scalar=ROUTE_SCALE,
                                 in1=r.inverse[:].unsqueeze(2).to_broadcast([P, TILES, EXPERTS]),
                                 op0=ALU.mult, op1=ALU.mult).then_inc(r.combine_ready, 1)


def turn_combine(pe, r, ident, dst, b):
    pe.wait_ge(r.combine_ready, b + 1)
    for t in range(TILES):
        last = pe.transpose(dst[0:EXPERTS, t * P:(t + 1) * P], r.combine[:, t, :], ident[:])
    last.then_inc(r.combine_turned, 1)


def copy_combine(act, r, src, b, first):
    act.wait_ge(r.combine_turned, b + 1)
    if not first:
        for loaded in r.weights_loaded:
            act.wait_ge(loaded, DMA * b)
    act.copy(r.combine_T[:], src[0:EXPERTS, :]).then_inc(r.combine_copied, 1)


def write_combine(sp, r, b):
    sp.wait_ge(r.combine_copied, b + 1)
    sp.dma_start(r.combine_rows, r.combine_T[:]).then_inc(r.combine_written, DMA)
    sp.wait_ge(r.combine_written, DMA * (b + 1))


def load_weights(sp, r, i):
    sp.dma_start(r.weights[:, 4 * i:4 * i + 4, :],
                 r.combine_rows[4 * i:4 * i + 4, :].unsqueeze(0).to_broadcast([P, 4, SEQ])
                 ).then_inc(r.weights_loaded[i], DMA)


def attention(nc, r, c, stream, nets_high, nets_low, ident, x_tiles, xT, w_qkv, w_nets,
              gate_wT, expert_bias, q_rows, k_rows, shift_rows):
    with ExitStack() as ctx:
        def sb(name, shape, dt=F32):
            return ctx.enter_context(nc.sbuf_tensor(name, shape, dt))

        def psum(name, shape):
            return ctx.enter_context(nc.psum_tensor(name, shape, F32))

        def sem(name):
            return ctx.enter_context(nc.semaphore(name))

        q_pad = sb("q_pad", [P, GROUPS, GROUP, SEQ], F32R)
        k_aug = sb("k_aug", [P, GROUPS, SEQ], F32R)
        v_ones = sb("v_ones", [P, GROUPS, TILES, GROUP, 32])
        probs = sb("probs", [P, 2, GROUP, SEQ])
        xT_sb = sb("xT_sb", [P, SEQ])
        w_sb = sb("w_sb", [P, 3 * HIDDEN])
        qk_raw = sb("qk_raw", [P, 2, SEQ])
        qk_high = sb("qk_high", [P, 2, SEQ], F32R)
        qk_low = sb("qk_low", [P, 2, SEQ], F32R)
        v_stage = sb("v_stage", [P, TILES, HIDDEN])
        maxima = sb("maxima", [P, 2, GROUP * TILES])
        shift_raw = sb("shift_raw", [GROUP * TILES, P])
        shift = sb("shift", [GROUP * TILES, 2, P], F32R)
        net_raw = sb("net_raw", [P, 3 * P])


        ps_q = [psum(f"ps_q{i}", [P, SEQ]) for i in range(3)]
        ps_k = [psum(f"ps_k{i}", [P, SEQ]) for i in range(3)]
        ps_ctx = psum("ps_ctx", [P, SEQ])
        ps_misc = c.ps_turned

        xT_loaded = sem("xT_loaded")
        w_loaded = sem("w_loaded")
        stream_loaded = sem("stream_loaded")
        pads_set = sem("pads_set")
        q_pads_set = sem("q_pads_set")
        v_pads_set = sem("v_pads_set")
        pads_written = sem("pads_written")
        ident_zeroed = sem("ident_zeroed")
        ident_set = sem("ident_set")
        qk_projected = sem("qk_projected")
        qk_highs = sem("qk_highs")
        qk_split = sem("qk_split")
        v_projected = sem("v_projected")
        v_staged = sem("v_staged")
        v_placed = sem("v_placed")
        rows_written = sem("rows_written")
        slot_loaded = [sem(f"slot_loaded{g}") for g in range(GROUPS)]
        heads_loaded = sem("heads_loaded")
        scores_q = sem("scores_q")
        scores_q_used = sem("scores_q_used")
        maxima_turned = sem("maxima_turned")
        shift_high = sem("shift_high")
        shift_split = sem("shift_split")
        shift_written = sem("shift_written")
        shift_loaded = sem("shift_loaded")
        scores_k = sem("scores_k")
        exp_done = sem("exp_done")
        context_step = sem("context_step")
        net_loaded = sem("net_loaded")
        net_high = sem("net_high")
        net_split = sem("net_split")

        block = ctx.enter_context(nc.Block())

        @block.sync
        def _(sp):
            def load_xT(column):
                sp.dma_start(xT_sb[:], xT[:, bass.ds(column, SEQ)]).then_inc(xT_loaded, DMA)

            def load_slot(g, first=False):
                sp.dma_start(k_aug[:, g, :].bitcast(F32),
                             k_rows[g * GROUP:(g + 1) * GROUP].rearrange("h r s -> (h r) s")
                             ).then_inc(slot_loaded[g], DMA)
                for h in range(GROUP):
                    sp.dma_start(q_pad[h * ROWS:(h + 1) * ROWS, g, h, :].bitcast(F32),
                                 q_rows[g * GROUP + h]
                                 ).then_inc(heads_loaded if first and h > 0 else slot_loaded[g], DMA)

            def write_rows(b):
                def write(rows, part, i, r):
                    sp.dma_start(rows[:, r * HEAD:(r + 1) * HEAD, :], part[:, i, :].bitcast(F32)
                                 ).then_inc(rows_written, DMA)

                sp.wait_ge(qk_highs, 2 * b + 1)
                write(q_rows, qk_high, 0, 0)
                write(q_rows, qk_high, 0, 2)
                sp.wait_ge(qk_split, 2 * b + 1)
                write(q_rows, qk_low, 0, 1)
                sp.wait_ge(qk_highs, 2 * b + 2)
                write(k_rows, qk_high, 1, 0)
                write(k_rows, qk_high, 1, 1)
                sp.wait_ge(qk_split, 2 * b + 2)
                write(k_rows, qk_low, 1, 2)

            def spread_shift(u, g):
                sp.wait_ge(shift_split, u + 1)
                sp.dma_start(shift_rows.rearrange("c m q -> m c q"),
                             shift[:].bitcast(F32)).then_inc(shift_written, DMA)
                sp.wait_ge(shift_written, DMA * (u + 1))
                for h in range(GROUP):
                    r = h * ROWS + SHIFT_ROW
                    sp.dma_start(q_pad[r:r + 2, g, h, :].bitcast(F32),
                                 shift_rows[:, h * TILES:(h + 1) * TILES, :].rearrange("c t q -> c (t q)")
                                 ).then_inc(shift_loaded, DMA)

            def body(b, first=False, last=False):
                for g in range(GROUPS):
                    u = GROUPS * b + g
                    if g == 0 and not last:
                        column = (b + 1) * SEQ
                        if not first:
                            column = sp.snap(column)
                        sp.wait_ge(v_projected, b + 1)
                        load_xT(column)
                    if not last or g == 0:
                        if not (first and g == 0):
                            sp.wait_ge(scores_k, UNIT * u)
                        if g > 0:
                            sp.wait_ge(rows_written, 6 * DMA * (b + 2))
                        load_slot((g + 3) % GROUPS)
                    if not last or g < GROUPS - 1:
                        spread_shift(u + 1, (g + 1) % GROUPS)
                    if g == 0 and not last:
                        sp.wait_ge(slot_loaded[3], slot_loads(3, b + 1))
                        write_rows(b + 1)

            load_xT(0)
            sp.dma_start(w_sb[:], w_qkv).then_inc(w_loaded, DMA)
            sp.wait_ge(pads_set, 2)
            sp.dma_start(q_rows[:, SHIFT_ROW:ROWS, :], q_pad[:, 0, 0, :].bitcast(F32)).then_inc(pads_written, DMA)
            sp.dma_start(k_rows[:, SHIFT_ROW:ROWS, :], k_aug[:, 0, :].bitcast(F32)).then_inc(pads_written, DMA)
            write_rows(0)
            sp.wait_ge(pads_written, 2 * DMA)
            sp.wait_ge(rows_written, 6 * DMA)
            load_slot(0, first=True)
            sp.wait_ge(q_pads_set, 1)
            load_slot(1)
            load_slot(2)
            for c in range(4):
                n = BATCHES * TILES // 4
                sp.dma_start(stream[:, c * n:(c + 1) * n, :], x_tiles[:, c * n:(c + 1) * n, :]
                             ).then_inc(stream_loaded, DMA)
            sp.dma_start(r.gate_w[:], gate_wT).then_inc(r.consts_loaded, DMA)
            sp.dma_start(r.bias[:], expert_bias.unsqueeze(0).to_broadcast([P, EXPERTS])
                         ).then_inc(r.consts_loaded, DMA)
            spread_shift(0, 0)
            body(0, first=True)
            with sp.Fori(1, BATCHES - 1) as b:
                body(b)
            body(BATCHES - 1, last=True)
            write_combine(sp, r, 0)
            for i in range(4):
                load_weights(sp, r, i)

        @block.gpsimd
        def _(pool):
            def place_v(u, g):
                at = V_COLUMN[g % PAIR]
                pool.tensor_tensor(v_ones[:, g, :, :, at:at + HEAD],
                                   v_stage[:, :, g * GROUP * HEAD:(g + 1) * GROUP * HEAD]
                                   .rearrange("p t (h e) -> p t h e", h=GROUP),
                                   r.ones[:, 0:HIDDEN].rearrange("p (t h e) -> p t h e", t=TILES, h=GROUP),
                                   ALU.mult).then_inc(v_placed, 1)

            def split_net(e):
                pool.dma_start(net_raw[:], w_nets[:, bass.ds(e * 3 * P, 3 * P)]).then_inc(net_loaded, DMA)
                high = nets_high[:, bass.ds(e, 1), :, :].rearrange("p a b c -> p (a b c)")
                low = nets_low[:, bass.ds(e, 1), :, :].rearrange("p a b c -> p (a b c)")
                pool.wait_ge(net_loaded, DMA * (e + 1))
                pool.tensor_tensor(high, net_raw[:], r.ones[:, 0:3 * P], ALU.mult).then_inc(net_high, 1)
                pool.wait_ge(net_high, e + 1)
                pool.tensor_tensor(low, net_raw[:], high.bitcast(F32), ALU.subtract).then_inc(net_split, 1)
                pool.wait_ge(net_split, e + 1)

            def body(b, first=False, last=False):
                for g in range(GROUPS):
                    u = GROUPS * b + g
                    if not (first and g == 0) and not (last and g > 0):
                        pool.wait_ge(context_step, 4 * u)
                        pool.wait_ge(v_staged, b + 1 if g == 0 else b + 2)
                        place_v(u + 3, (g + 3) % GROUPS)
                    if g == 1 and not first:
                        add_context(pool, c, stream, 2 * b - 1, b - 1, 1)
                    if g == 3:
                        add_context(pool, c, stream, 2 * b, b, 0)
                    if first:
                        for e in ((0, 1), (2,), (3,), (4,))[g]:
                            split_net(e)
                    elif not last and g in (1, 3):
                        split_net(2 * b + 3 + g // 2)
                    elif last and g == 2:
                        take_scale(pool, r, 0, 0)
                        keep_x1(pool, r, stream, 0)

            pool.memset(q_pad[:, 1:, :, :].rearrange("p a b c -> p (a b c)").bitcast(F32), 0.0
                        ).then_inc(q_pads_set, 1)
            pool.memset(ident[:], 0.0).then_inc(ident_zeroed, 1)
            pool.wait_ge(ident_zeroed, 1)
            pool.affine_select(out=ident[:], in_=ident[:], compare_op=ALU.not_equal, fill=1.0,
                               base=0, pattern=[[-1, P]], channel_multiplier=1).then_inc(ident_set, 1)
            pool.memset(v_ones[:].rearrange("p a b c d -> p (a b c d)"), 0.0).then_inc(v_pads_set, 1)
            pool.wait_ge(v_pads_set, 1)
            for g in range(GROUPS):
                at = V_COLUMN[g % PAIR] + HEAD
                pool.memset(v_ones[:, g, :, :, at:at + 1], 1.0).then_inc(v_pads_set, 1)
            pool.memset(r.ones[:], 1.0).then_inc(r.consts_set, 1)
            pool.memset(r.minus_half[:], -0.5).then_inc(r.consts_set, 1)
            pool.memset(r.epsilon[:], EPS).then_inc(r.consts_set, 1)
            pool.wait_ge(v_pads_set, 1 + GROUPS)
            pool.wait_ge(r.consts_set, 3)
            pool.wait_ge(v_staged, 1)
            for g in range(GROUPS):
                place_v(g, g)
            pool.wait_ge(stream_loaded, 4 * DMA)
            body(0, first=True)
            with pool.Fori(1, BATCHES - 1) as b:
                body(b)
            body(BATCHES - 1, last=True)

        @block.scalar
        def _(act):
            def copy_context(pair, wait_turned):
                act.wait_ge(context_step, 4 * PAIR * (pair + 1))
                if wait_turned:
                    act.wait_ge(c.turned, pair)
                act.copy(c.context_T[:], ps_ctx[:]).then_inc(c.copied, 1)

            def round_shift(u, first):
                act.wait_ge(maxima_turned, u + 1)
                if not first:
                    act.wait_ge(shift_loaded, GROUP * DMA * u)
                act.copy(shift_raw[:], ps_misc[0:GROUP * TILES, 0:P])
                act.copy(shift[:, 0, :], ps_misc[0:GROUP * TILES, 0:P]).then_inc(shift_high, 1)

            def round_qk(b, i, src, first):
                act.wait_ge(qk_projected, 2 * b + i + 1)
                if not first:
                    act.wait_ge(rows_written, 6 * DMA * b)
                act.copy(qk_raw[:, i, :], src[:])
                act.copy(qk_high[:, i, :], src[:]).then_inc(qk_highs, 1)

            def stage_v(b, src, first):
                act.wait_ge(v_projected, b + 1)
                if not first:
                    act.wait_ge(v_placed, GROUPS * b)
                act.copy(v_stage[:].rearrange("p t d -> p (t d)"), src[:]).then_inc(v_staged, 1)

            def body(b, first=False, last=False):
                for g in range(GROUPS):
                    u = GROUPS * b + g
                    for t in range(TILES):
                        for h in range(GROUP):
                            i = UNIT * g + 4 * t + h
                            if h == 0 and not (first and g == 0 and t < 2):
                                act.wait_ge(context_step, 4 * u + t - 1)
                            act.wait_ge(scores_k, SCORES * b + i + 1)
                            act.activation(probs[:, t % 2, h, :], ps_k[SCORE_SLOT[i]][:], ACT.Exp,
                                           scale=ATT_SCALE).then_inc(exp_done, 1)
                            if (t, h) == (0, 3) and not (last and g == GROUPS - 1):
                                round_shift(u + 1, False)
                            if (t, h) == (1, 0) and g == 0 and not first:
                                copy_context(2 * b - 1, True)
                            if (t, h) == (1, 0) and g == 2:
                                copy_context(2 * b, not first)
                            if (t, h) == (1, 3) and g == 0 and not last:
                                round_qk(b + 1, 0, ps_misc, False)
                            if (t, h) == (2, 3) and g == 0 and not last:
                                round_qk(b + 1, 1, ps_misc, False)
                            if (g, t, h) == (2, 2, 1) and last:
                                copy_x1T(act, r, ps_misc, 0, True)
                            if (g, t, h) == (2, 2, 3) and last:
                                act.wait_ge(r.x1T_ready, 1)
                                round_x1T(act, r)
                            if (g, t, h) == (2, 3, 3) and last:
                                decay_gates(act, r, ps_misc, 0)
                            if (g, t, h) == (3, 1, 3) and last:
                                copy_combine(act, r, ps_misc, 0, True)
                            if (t, h) == (3, 2) and g == 0 and not last:
                                stage_v(b + 1, ps_misc, False)

            round_qk(0, 0, ps_misc, True)
            round_qk(0, 1, ps_ctx, True)
            stage_v(0, ps_k[0], True)
            round_shift(0, True)
            body(0, first=True)
            with act.Fori(1, BATCHES - 1) as b:
                body(b)
            body(BATCHES - 1, last=True)
            copy_context(2 * BATCHES - 1, True)

        @block.vector
        def _(dve):
            def take_maximum(u, b, i, parity, wait_turned):
                if wait_turned:
                    dve.wait_ge(maxima_turned, u - 1)
                dve.wait_ge(scores_q, SCORES * b + i + 1)
                dve.tensor_reduce(maxima[:, parity, i % UNIT:i % UNIT + 1], ps_q[SCORE_SLOT[i % SCORES]][:],
                                  AX_X, ALU.max).then_inc(scores_q_used, 1)

            def split_shift(u):
                dve.wait_ge(shift_high, u + 1)
                dve.tensor_tensor(shift[:, 1, :], shift_raw[:],
                                  shift[:, 0, :].bitcast(F32), ALU.subtract).then_inc(shift_split, 1)

            def split_qk(b, i):
                dve.wait_ge(qk_highs, 2 * b + i + 1)
                dve.tensor_tensor(qk_low[:, i, :], qk_raw[:, i, :], qk_high[:, i, :].bitcast(F32),
                                  ALU.subtract).then_inc(qk_split, 1)

            def body(b, first=False, last=False):
                for g in range(GROUPS):
                    u = GROUPS * b + g
                    maxima_of_next = not last or g < AHEAD
                    for i in range(UNIT):
                        if maxima_of_next:
                            take_maximum(u + AHEAD, b, UNIT * (g + AHEAD) + i, g % 2, i == 0)
                        if i == 3 and not (last and g == GROUPS - 1):
                            split_shift(u + 1)
                        if i == 11 and g == 1 and not first:
                            normalise_context(dve, c, 2 * b - 1, True)
                        if i == 11 and g == 3:
                            normalise_context(dve, c, 2 * b, not first)
                        if i == 9 and g == 0 and not last:
                            split_qk(b + 1, 0)
                        if i == 13 and g == 0 and not last:
                            split_qk(b + 1, 1)
                        if i == 0 and g == 2 and last:
                            take_moments(dve, r, stream_tile(stream, 0), 0)
                            normalise_stream(dve, r, stream, 0, True)
                        if i == 11 and g == 2 and last:
                            split_x1T(dve, r, 0)
                            for part in range(3):
                                select_experts(dve, r, 0, part)

            dve.memset(k_aug[:, 0, :].bitcast(F32), -1.0).then_inc(pads_set, 1)
            dve.memset(q_pad[:, 0, :, :].rearrange("p b c -> p (b c)").bitcast(F32), 0.0).then_inc(pads_set, 1)
            split_qk(0, 0)
            split_qk(0, 1)
            for u in range(AHEAD):
                for i in range(UNIT):
                    take_maximum(u, 0, UNIT * u + i, u, False)
                if u == 0:
                    split_shift(0)
            body(0, first=True)
            with dve.Fori(1, BATCHES - 1) as b:
                body(b)
            body(BATCHES - 1, last=True)

        @block.tensor
        def _(pe):
            def score_q(i):
                g, h, t = i // UNIT, i // 4 % 4, i % 4
                return pe.matmul(ps_q[SCORE_SLOT[i]][:], q_pad[:, g, h, t * P:(t + 1) * P],
                                 k_aug[:, g, :], start=True, stop=True).then_inc(scores_q, 1)

            def score_k(i):
                g, t, h = i // UNIT, i // 4 % 4, i % 4
                return pe.matmul(ps_k[SCORE_SLOT[i]][:], k_aug[:, g, t * P:(t + 1) * P], q_pad[:, g, h, :],
                                 start=True, stop=True).then_inc(scores_k, 1)

            def weigh_values(u, g, t, pairs_before):
                pe.wait_ge(exp_done, UNIT * u + GROUP * (t + 1))
                opens = t == 0 and g % PAIR == 0
                closes = t == TILES - 1 and g % PAIR == PAIR - 1
                if t == 0:
                    pe.wait_ge(v_placed, u + 1)
                    if opens and pairs_before is not None:
                        pe.wait_ge(c.copied, pairs_before)
                for h in range(GROUP):
                    last = pe.matmul(ps_ctx[32 * h:32 * (h + 1), :], v_ones[:, g, t, h, :],
                                     probs[:, t % 2, h, :], start=opens, stop=closes)
                last.then_inc(context_step, 1)

            def turn_maxima(u, parity):
                pe.wait_ge(scores_q_used, UNIT * (u + 1))
                pe.transpose(ps_misc[0:GROUP * TILES, 0:P], maxima[:, parity, :], ident[:]
                             ).then_inc(maxima_turned, 1)

            def project_qk(i, dst):
                pe.matmul(dst[:], w_sb[:, i * HIDDEN:(i + 1) * HIDDEN], xT_sb[:],
                          start=True, stop=True).then_inc(qk_projected, 1)

            def project_v(dst):
                for t in range(TILES):
                    last = pe.matmul(dst[:, t * P:(t + 1) * P], xT_sb[:, t * P:(t + 1) * P],
                                     w_sb[:, 2 * HIDDEN:3 * HIDDEN], start=True, stop=True)
                last.then_inc(v_projected, 1)

            def body(b, first=False, last=False):
                for g in range(GROUPS):
                    u = GROUPS * b + g
                    begun = not (first and g == 0)
                    maxima_of_next = not last or g < AHEAD
                    more = not last or g < GROUPS - 1
                    project = g == 0 and not last
                    g_next = (g + AHEAD) % GROUPS
                    for t in range(TILES):
                        for h in range(GROUP):
                            if (t, h) == (0, 0):
                                pe.wait_ge(shift_loaded, GROUP * DMA * (u + 1))
                            i = UNIT * g + 4 * t + h
                            before = slot_user_before(i)
                            if not first or before >= 0:
                                pe.wait_ge(exp_done, SCORES * b + before + 1)
                            score_k(i)
                            if maxima_of_next:
                                if (t, h) == (0, 0):
                                    pe.wait_ge(slot_loaded[g_next], slot_loads(g_next, b + 1 + (g + AHEAD) // GROUPS))
                                over, i = divmod(i + UNIT * AHEAD, SCORES)
                                before = slot_user_before(i)
                                pe.wait_ge(scores_q_used, SCORES * (b + over) + before + 1)
                                score_q(i)
                            if (t, h) == (1, 2) and project:
                                pe.wait_ge(shift_high, u + 2)
                                pe.wait_ge(xT_loaded, DMA * (b + 2))
                                project_qk(0, ps_misc)
                            if (g, t, h) == (2, 2, 0) and last:
                                pe.wait_ge(shift_high, u + 2)
                                turn_x1(pe, r, ident, ps_misc, 0)
                            if (g, t, h) == (2, 3, 2) and last:
                                pe.wait_ge(r.consts_loaded, 2 * DMA)
                                gate(pe, r, ps_misc, 0)
                            if (g, t, h) == (3, 1, 2) and last:
                                turn_combine(pe, r, ident, ps_misc, 0)
                            if (t, h) == (2, 2) and project:
                                pe.wait_ge(qk_highs, 2 * b + 3)
                                project_qk(1, ps_misc)
                            if (t, h) == (0, 2) and more:
                                if g == 0 and not first:
                                    pe.wait_ge(c.ready, 2 * b - 1)
                                elif g == 1 and not last:
                                    pe.wait_ge(v_staged, b + 2)
                                elif g == 2 and not first:
                                    pe.wait_ge(c.ready, 2 * b)
                                else:
                                    pe.wait_ge(shift_high, u + 1)
                                turn_maxima(u + 1, (g + 1) % 2)
                            if (t, h) == (3, 1) and project:
                                pe.wait_ge(qk_highs, 2 * b + 4)
                                project_v(ps_misc)
                            if (t, h) == (2, 1) and (g == 3 or g == 1 and not first):
                                if last and g == 3:
                                    pe.wait_ge(r.combine_copied, 1)
                                else:
                                    pe.wait_ge(shift_high, u + 2)
                                turn_context(pe, c, ident, 2 * b - 1 if g == 1 else 2 * b)
                        if t > 0:
                            weigh_values(u, g, t - 1, None if first and g < PAIR else 2 * b + g // PAIR)
                        elif begun:
                            weigh_values(u - 1, (g + 3) % GROUPS, TILES - 1, None)

            pe.wait_ge(xT_loaded, DMA)
            pe.wait_ge(w_loaded, DMA)
            project_qk(0, ps_misc)
            project_qk(1, ps_ctx)
            project_v(ps_k[0])
            for u in range(AHEAD):
                pe.wait_ge(slot_loaded[u], slot_loads(u, 1))
                for i in range(UNIT * u, UNIT * (u + 1)):
                    if i == 4:
                        pe.wait_ge(heads_loaded, DMA * (GROUP - 1))
                    if i >= 3:
                        pe.wait_ge(scores_q_used, slot_user_before(i) + 1)
                    score_q(i)
                if u == 0:
                    pe.wait_ge(ident_set, 1)
                    pe.wait_ge(v_staged, 1)
                    turn_maxima(0, 0)
            body(0, first=True)
            with pe.Fori(1, BATCHES - 1) as b:
                body(b)
            body(BATCHES - 1, last=True)
            weigh_values(UNITS - 1, GROUPS - 1, TILES - 1, None)


def feed_forward(nc, r, c, stream, nets_high, nets_low, ident, out_tiles):
    STEPS = NETS + 1
    LAG = 4
    UP_RING = 3
    RING = 6
    LAST = NETS - 1

    def before(s, ring):
        n = s - ring
        while n < 0 and n + STEPS > LAST:
            n -= ring
        return (0, n) if n >= 0 else (-1, n + STEPS)

    with ExitStack() as ctx:
        def sb(name, shape, dt=F32):
            return ctx.enter_context(nc.sbuf_tensor(name, shape, dt))

        def psum(name, shape):
            return ctx.enter_context(nc.psum_tensor(name, shape, F32))

        def sem(name):
            return ctx.enter_context(nc.semaphore(name))

        silu = sb("silu", [P, UP_RING, SEQ])
        gated = sb("gated", [P, UP_RING, SEQ])
        hidden = sb("hidden", [P, RING, SEQ])
        hidden_high = sb("hidden_high", [P, RING, SEQ], F32R)
        hidden_low = sb("hidden_low", [P, RING, SEQ], F32R)
        yT = sb("yT", [P, SEQ])
        y_sum = sb("y_sum", [P, TILES, HIDDEN])
        result = sb("result", [P, TILES, HIDDEN])

        ps_gate = [psum("ps_gate0", [P, SEQ]), psum("ps_gate1", [P, SEQ])]
        ps_up = [psum(f"ps_up{i}", [P, SEQ]) for i in range(UP_RING)]
        ps_y = psum("ps_y", [P, SEQ])
        ps_route = psum("ps_route", [P, SEQ])
        ps_out = c.ps_turned

        gate_ready = sem("gate_ready")
        up_ready = sem("up_ready")
        silu_done = sem("silu_done")
        gated_done = sem("gated_done")
        hidden_done = sem("hidden_done")
        hidden_highs = sem("hidden_highs")
        hidden_split = sem("hidden_split")
        down_done = sem("down_done")
        y_copied = sem("y_copied")
        y_turned = sem("y_turned")
        y_summed = sem("y_summed")
        result_ready = sem("result_ready")
        stored = sem("stored")

        block = ctx.enter_context(nc.Block())

        LN_IN, TURN_X1, COPY_X1T, GATE, ROUTE, TURN_COMBINE, COPY_COMBINE = 1, 5, 5, 6, 7, 14, 14
        COPY_Y, TURN_Y, SUM_Y, LN_OUT = 3, 5, 6, 13

        @block.sync
        def _(sp):
            def store(b):
                tile = b * TILES if isinstance(b, int) else sp.snap(b * TILES)
                sp.wait_ge(result_ready, b + 1)
                sp.dma_start(out_tiles[:, bass.ds(tile, TILES), :], result[:]).then_inc(stored, DMA)

            def body(b, first=False, last=False):
                if not first:
                    store(b - 1)
                if not last:
                    write_combine(sp, r, b + 1)
                    for i in range(4):
                        sp.wait_ge(hidden_done, EXPERTS * b + 4 * (i + 1))
                        load_weights(sp, r, i)

            body(0, first=True)
            with sp.Fori(1, BATCHES - 1) as b:
                body(b)
            body(BATCHES - 1, last=True)
            store(BATCHES - 1)
            sp.wait_ge(stored, DMA * BATCHES)

        @block.gpsimd
        def _(pool):
            def body(b, first=False, last=False):
                for s in range(STEPS):
                    if 1 <= s <= LAST:
                        e = s - 1
                        if e % 4 == 0:
                            pool.wait_ge(r.weights_loaded[e // 4], DMA * (b + 1))
                        pool.wait_ge(gated_done, NETS * b + s + 1)
                        db, n = before(s, RING)
                        if not (first and db < 0):
                            pool.wait_ge(hidden_split, NETS * (b + db) + n + 1)
                        pool.tensor_tensor(hidden[:, s % RING, :], gated[:, s % UP_RING, :], r.weights[:, e, :],
                                           ALU.mult).then_inc(hidden_done, 1)
                    if s == LN_IN and not last:
                        take_scale(pool, r, b + 1, 0)
                    if s == LN_IN + 2 and not last:
                        keep_x1(pool, r, stream, b + 1)
                    if s == SUM_Y + 1 and not first:
                        take_scale(pool, r, b - 1, 1)

            add_context(pool, c, stream, 2 * BATCHES - 1, BATCHES - 1, 1)
            body(0, first=True)
            with pool.Fori(1, BATCHES - 1) as b:
                body(b)
            body(BATCHES - 1, last=True)
            take_scale(pool, r, BATCHES - 1, 1)

        @block.scalar
        def _(act):
            def copy_y(b):
                act.wait_ge(down_done, NETS * (b + 1))
                act.copy(yT[:], ps_y[:]).then_inc(y_copied, 1)

            def round_hidden(b, n, first):
                if n == 0:
                    act.wait_ge(gated_done, NETS * b + 1)
                else:
                    act.wait_ge(hidden_done, EXPERTS * b + n)
                db, m = before(n, RING)
                if not (first and db < 0):
                    act.wait_ge(down_done, NETS * (b + db) + m + 1)
                act.copy(hidden_high[:, n % RING, :], hidden[:, n % RING, :]).then_inc(hidden_highs, 1)

            def body(b, first=False, last=False):
                for s in range(STEPS):
                    if s <= LAST:
                        act.wait_ge(gate_ready, NETS * b + s + 1)
                        db, n = before(s, UP_RING)
                        if not (first and db < 0):
                            act.wait_ge(gated_done, NETS * (b + db) + n + 1)
                        act.activation(silu[:, s % UP_RING, :], ps_gate[s % 2][:], ACT.Silu).then_inc(silu_done, 1)
                    if s == STEPS - 1 and not last:
                        act.wait_ge(up_ready, NETS * (b + 1))
                        if not first:
                            act.wait_ge(stored, DMA * b)
                        round_x1T(act, r)
                    if s >= 2:
                        round_hidden(b, s - 2, first)
                    elif s == 0 and not first:
                        round_hidden(b - 1, LAST, False)
                    if s == COPY_Y and not first:
                        copy_y(b - 1)
                    if s == COPY_X1T and not last:
                        copy_x1T(act, r, ps_route, b + 1, False)
                    if s == COPY_COMBINE and not last:
                        copy_combine(act, r, ps_route, b + 1, False)
                    if s == GATE + 1 and not last:
                        decay_gates(act, r, ps_route, b + 1)

            body(0, first=True)
            with act.Fori(1, BATCHES - 1) as b:
                body(b)
            body(BATCHES - 1, last=True)
            round_hidden(BATCHES - 1, LAST, False)
            copy_y(BATCHES - 1)

        @block.vector
        def _(dve):
            def sum_y(b):
                dve.wait_ge(y_turned, b + 1)
                dve.wait_ge(r.x1_kept, b + 1)
                dve.tensor_tensor(y_sum[:], ps_out[:].rearrange("p (t d) -> p t d", t=TILES),
                                  stream[:, bass.ds(b * TILES, TILES), :], ALU.add).then_inc(y_summed, 1)
                dve.drain()
                take_moments(dve, r, lambda t: y_sum[:, t, :], 1)

            def finish(b):
                normalise(dve, r, result, lambda t: y_sum[:, t, :], b, 1, result_ready)

            def gate_up(b, s, first):
                dve.wait_ge(silu_done, NETS * b + s + 1)
                dve.wait_ge(up_ready, NETS * b + s + 1)
                if s == 0:
                    db, n = before(0, RING)
                    if not first:
                        dve.wait_ge(hidden_split, NETS * (b + db) + n + 1)
                    dst = hidden[:, 0, :]
                else:
                    db, n = before(s, UP_RING)
                    if n > 0 and not (first and db < 0):
                        dve.wait_ge(hidden_done, EXPERTS * (b + db) + n)
                    dst = gated[:, s % UP_RING, :]
                dve.tensor_tensor(dst, silu[:, s % UP_RING, :], ps_up[s % UP_RING][:], ALU.mult).then_inc(gated_done, 1)

            def split_hidden(b, n, first):
                dve.wait_ge(hidden_highs, NETS * b + n + 1)
                dve.tensor_tensor(hidden_low[:, n % RING, :], hidden[:, n % RING, :],
                                  hidden_high[:, n % RING, :].bitcast(F32), ALU.subtract
                                  ).then_inc(hidden_split, 1)

            def body(b, first=False, last=False):
                for s in range(STEPS):
                    if s <= LAST:
                        gate_up(b, s, first)
                    if s == STEPS - 1 and not last:
                        split_x1T(dve, r, b + 1)
                    if s >= 2:
                        split_hidden(b, s - 2, first)
                    elif s == 0 and not first:
                        split_hidden(b - 1, LAST, False)
                    if s == LN_IN - 1 and not last:
                        take_moments(dve, r, stream_tile(stream, b + 1), 0)
                    if s == LN_IN + 1 and not last:
                        normalise_stream(dve, r, stream, b + 1, False)
                    if s in (ROUTE, ROUTE + 2, ROUTE + 4) and not last:
                        select_experts(dve, r, b + 1, (s - ROUTE) // 2)
                    if s == SUM_Y and not first:
                        sum_y(b - 1)
                    if s == LN_OUT and not first:
                        finish(b - 1)

            normalise_context(dve, c, 2 * BATCHES - 1, True)
            body(0, first=True)
            with dve.Fori(1, BATCHES - 1) as b:
                body(b)
            body(BATCHES - 1, last=True)
            split_hidden(BATCHES - 1, LAST, False)
            sum_y(BATCHES - 1)
            dve.wait_ge(stored, DMA * (BATCHES - 1))
            finish(BATCHES - 1)

        @block.tensor
        def _(pe):
            def three_passes(dst, n, j, high, low, start, stop):
                pe.matmul(dst, nets_low[:, n, j, :], high, start=start, stop=False)
                pe.matmul(dst, nets_high[:, n, j, :], high, start=False, stop=False)
                return pe.matmul(dst, nets_high[:, n, j, :], low, start=False, stop=stop)

            def gate_up(b, s, first):
                if s == 0:
                    pe.wait_ge(r.x1T_highs, b + 1)
                db, n = before(s, 2)
                if not (first and db < 0):
                    pe.wait_ge(silu_done, NETS * (b + db) + n + 1)

                def low_weights(j, dst):
                    pe.matmul(dst[:], nets_low[:, s, j, :], r.x1T_high[:], start=True, stop=False)

                def high_weights(j, dst, x, stop):
                    return pe.matmul(dst[:], nets_high[:, s, j, :], x[:], start=False, stop=stop)

                ps_g, ps_u = ps_gate[s % 2], ps_up[s % UP_RING]
                low_weights(0, ps_g)
                high_weights(0, ps_g, r.x1T_high, False)
                if s > 0:
                    high_weights(0, ps_g, r.x1T_low, True).then_inc(gate_ready, 1)
                db, n = before(s, UP_RING)
                if not (first and db < 0):
                    pe.wait_ge(gated_done, NETS * (b + db) + n + 1)
                low_weights(1, ps_u)
                high_weights(1, ps_u, r.x1T_high, False)
                if s == 0:
                    pe.wait_ge(r.x1T_split, b + 1)
                    high_weights(0, ps_g, r.x1T_low, True).then_inc(gate_ready, 1)
                high_weights(1, ps_u, r.x1T_low, True).then_inc(up_ready, 1)

            def down(b, n, first):
                pe.wait_ge(hidden_split, NETS * b + n + 1)
                if n == 0 and not first:
                    pe.wait_ge(y_copied, b)
                three_passes(ps_y[:], n, 2, hidden_high[:, n % RING, :], hidden_low[:, n % RING, :],
                             n == 0, n == LAST).then_inc(down_done, 1)

            def turn_y(b):
                pe.wait_ge(y_copied, b + 1)
                for t in range(TILES):
                    last = pe.transpose(ps_out[:, t * P:(t + 1) * P], yT[:, t * P:(t + 1) * P], ident[:])
                last.then_inc(y_turned, 1)

            def body(b, first=False, last=False):
                for s in range(STEPS):
                    if s <= LAST:
                        gate_up(b, s, first)
                    if s >= LAG:
                        down(b, s - LAG, first)
                    elif s < LAG - 1 and not first:
                        down(b - 1, s + STEPS - LAG, False)
                    if s == TURN_X1 and not last:
                        pe.wait_ge(r.combine_copied, b + 1)
                        turn_x1(pe, r, ident, ps_route, b + 1)
                    if s == TURN_Y and not first:
                        turn_y(b - 1)
                    if s == GATE and not last:
                        gate(pe, r, ps_route, b + 1)
                    if s == TURN_COMBINE and not last:
                        turn_combine(pe, r, ident, ps_route, b + 1)

            turn_context(pe, c, ident, 2 * BATCHES - 1)
            body(0, first=True)
            with pe.Fori(1, BATCHES - 1) as b:
                body(b)
            body(BATCHES - 1, last=True)
            for n in range(STEPS - LAG, NETS):
                down(BATCHES - 1, n, False)
            turn_y(BATCHES - 1)


def kernel(**inputs):
    import numpy as np
    import concourse.bacc as bacc
    from concourse.bass_utils import run_bass_kernel_spmd

    def array(name):
        return np.asarray(inputs[name])

    x = array("L0_attn_embeddings")
    gates = np.concatenate([array("L0_ffn_shared_gate_w")[None], array("L0_ffn_w_gate")]).transpose(2, 0, 1)
    ups = np.concatenate([array("L0_ffn_shared_up_w")[None], array("L0_ffn_w_up")]).transpose(2, 0, 1)
    downs = np.concatenate([array("L0_ffn_shared_down_w")[None], array("L0_ffn_w_down")]).transpose(2, 0, 1)
    arrays = {
        "x": x,
        "xT": x.reshape(-1, HIDDEN).T,
        "w_qkv": array("L0_attn_w_qkv"),
        "w_nets": np.stack([gates, ups, downs], axis=2).reshape(P, -1),
        "gate_wT": array("L0_ffn_gate_w").T,
        "expert_bias": array("L0_ffn_expert_bias"),
    }
    arrays = {name: np.ascontiguousarray(a) for name, a in arrays.items()}
    nc = bacc.Bacc("TRN2", target_bir_lowering=False, num_devices=1)
    args = [nc.dram_tensor(name, a.shape, mybir.dt.from_np(a.dtype), kind="ExternalInput").ap()
            for name, a in arrays.items()]
    out = nc.dram_tensor("out", x.shape, F32, kind="ExternalOutput").ap()
    build(nc, *args, out)
    r = run_bass_kernel_spmd(nc, [arrays], core_ids=[0])
    return r.results[0]["out"]
```
